# Optimizing a Trainium2 kernel written in Bass

```python
import numpy as np
import jax
import jax.numpy as jnp

def _softmax(x, axis=-1):
    return jax.nn.softmax(x, axis=axis)

def _gelu(x):
    return jax.nn.gelu(x, approximate=True)

def _silu(x):
    return jax.nn.silu(x)

def _sigmoid(x):
    return jax.nn.sigmoid(x)

def _layernorm(x, axis=-1, eps=1e-05):
    m = jnp.mean(x, axis=axis, keepdims=True)
    v = jnp.var(x, axis=axis, keepdims=True)
    return (x - m) / jnp.sqrt(v + eps)

def _scatter_add(tgt, idx, src, axis=0):
    return tgt.at[idx].add(src)

def _segment_sum(src, seg, n):
    return jax.ops.segment_sum(src, seg, n)
kernel_name = 'mk_prb_d1_jaxref_r4_d80e76'

def setup_inputs(seed: int=0):
    np.random.seed(seed)
    _w = jnp.asarray

    def _L0_attn_setup():
        import jax, jax.numpy as jnp
        import numpy as np
        import math
        DIM = 256
        NUM_HEADS = 16
        HEAD_DIM = DIM // NUM_HEADS
        LAYER_IDX = 12
        LAMBDA_INIT = 0.8 - 0.6 * math.exp(-0.3 * (LAYER_IDX - 1))
        LN_EPS = 1e-05
        key = jax.random.key(seed)
        ks = jax.random.split(key, 11)
        B, S = (2, 512)
        x = jax.random.normal(ks[0], (B, S, DIM), dtype=jnp.float32)
        s = 1.0 / math.sqrt(DIM)
        Wq = jax.random.normal(ks[1], (DIM, 2 * DIM), dtype=jnp.float32) * s
        Wk = jax.random.normal(ks[2], (DIM, 2 * DIM), dtype=jnp.float32) * s
        Wv = jax.random.normal(ks[3], (DIM, DIM), dtype=jnp.float32) * s
        Wo = jax.random.normal(ks[4], (DIM, DIM), dtype=jnp.float32) * s
        lambda_q1 = jax.random.normal(ks[5], (HEAD_DIM,), dtype=jnp.float32) * 0.1
        lambda_k1 = jax.random.normal(ks[6], (HEAD_DIM,), dtype=jnp.float32) * 0.1
        lambda_q2 = jax.random.normal(ks[7], (HEAD_DIM,), dtype=jnp.float32) * 0.1
        lambda_k2 = jax.random.normal(ks[8], (HEAD_DIM,), dtype=jnp.float32) * 0.1
        gamma = jnp.ones((DIM,), dtype=jnp.float32)
        beta = jnp.zeros((DIM,), dtype=jnp.float32)
        return {'x': x, 'Wq': Wq, 'Wk': Wk, 'Wv': Wv, 'Wo': Wo, 'lambda_q1': lambda_q1, 'lambda_k1': lambda_k1, 'lambda_q2': lambda_q2, 'lambda_k2': lambda_k2, 'gamma': gamma, 'beta': beta}
    _L0_attn_in = _L0_attn_setup()

    def _L0_ffn_setup():
        import jax, jax.numpy as jnp
        import numpy as np
        LATENT = 256
        LEAF_W = 64
        DEPTH = 4
        N_LEAVES = 2 ** DEPTH
        N_NODES = 2 ** DEPTH - 1
        B, S = (4, 512)

        def _fff_params(key, prefix):
            ks = jax.random.split(key, 4)
            d, h, l, n = (LATENT, LEAF_W, N_LEAVES, N_NODES)
            s_in = 1.0 / np.sqrt(d).astype(np.float32)
            s_h = 1.0 / np.sqrt(h).astype(np.float32)
            return {f'{prefix}_node_w': jax.random.normal(ks[0], (n, d), jnp.float32) * s_in, f'{prefix}_node_b': jax.random.normal(ks[1], (n,), jnp.float32) * s_in, f'{prefix}_w1': jax.random.normal(ks[2], (l, d, h), jnp.float32) * s_in, f'{prefix}_b1': jnp.zeros((l, h), jnp.float32), f'{prefix}_w2': jax.random.normal(ks[3], (l, h, d), jnp.float32) * s_h, f'{prefix}_b2': jnp.zeros((l, d), jnp.float32)}

        def _fff(x, node_w, node_b, w1, b1, w2, b2):
            Bx, Sx, D = x.shape
            xf = x.reshape(-1, D)
            N = xf.shape[0]
            cur = jnp.zeros((N,), jnp.int32)
            for _ in range(DEPTH):
                pw = node_w[cur]
                score = jnp.einsum('nd,nd->n', xf, pw) + node_b[cur]
                cur = 2 * cur + 1 + (score >= 0).astype(jnp.int32)
            leaf = cur - N_NODES
            sel = jax.nn.one_hot(leaf, N_LEAVES, dtype=xf.dtype)
            hidden_all = jax.nn.relu(jnp.einsum('nd,ldh->lnh', xf, w1) + b1[:, None, :])
            hidden = hidden_all * sel.T[:, :, None]
            out = jnp.einsum('lnh,lho->no', hidden, w2) + sel @ b2
            return out.reshape(Bx, Sx, D)
        key = jax.random.key(seed)
        kx, kq, kk, kv = jax.random.split(key, 4)
        inp = {'x': jax.random.normal(kx, (B, S, LATENT), jnp.float32)}
        inp.update(_fff_params(kq, 'q'))
        inp.update(_fff_params(kk, 'k'))
        inp.update(_fff_params(kv, 'v'))
        return inp
    _L0_ffn_in = _L0_ffn_setup()
    _d = {'L0_attn_x': _L0_attn_in['x'], 'L0_attn_Wq': _L0_attn_in['Wq'], 'L0_attn_Wk': _L0_attn_in['Wk'], 'L0_attn_Wv': _L0_attn_in['Wv'], 'L0_attn_Wo': _L0_attn_in['Wo'], 'L0_attn_lambda_q1': _L0_attn_in['lambda_q1'], 'L0_attn_lambda_k1': _L0_attn_in['lambda_k1'], 'L0_attn_lambda_q2': _L0_attn_in['lambda_q2'], 'L0_attn_lambda_k2': _L0_attn_in['lambda_k2'], 'L0_attn_gamma': _L0_attn_in['gamma'], 'L0_attn_beta': _L0_attn_in['beta'], 'L0_ffn_q_node_w': _L0_ffn_in['q_node_w'], 'L0_ffn_q_node_b': _L0_ffn_in['q_node_b'], 'L0_ffn_q_w1': _L0_ffn_in['q_w1'], 'L0_ffn_q_b1': _L0_ffn_in['q_b1'], 'L0_ffn_q_w2': _L0_ffn_in['q_w2'], 'L0_ffn_q_b2': _L0_ffn_in['q_b2'], 'L0_ffn_k_node_w': _L0_ffn_in['k_node_w'], 'L0_ffn_k_node_b': _L0_ffn_in['k_node_b'], 'L0_ffn_k_w1': _L0_ffn_in['k_w1'], 'L0_ffn_k_b1': _L0_ffn_in['k_b1'], 'L0_ffn_k_w2': _L0_ffn_in['k_w2'], 'L0_ffn_k_b2': _L0_ffn_in['k_b2'], 'L0_ffn_v_node_w': _L0_ffn_in['v_node_w'], 'L0_ffn_v_node_b': _L0_ffn_in['v_node_b'], 'L0_ffn_v_w1': _L0_ffn_in['v_w1'], 'L0_ffn_v_b1': _L0_ffn_in['v_b1'], 'L0_ffn_v_w2': _L0_ffn_in['v_w2'], 'L0_ffn_v_b2': _L0_ffn_in['v_b2']}
    _x0 = _d['L0_attn_x']
    _d['L0_attn_x'] = jax.random.normal(jax.random.fold_in(jax.random.key(seed), 1), (8, 1024, 256), dtype=_x0.dtype)
    del _x0
    return _d

def reference(L0_attn_x, L0_attn_Wq, L0_attn_Wk, L0_attn_Wv, L0_attn_Wo, L0_attn_lambda_q1, L0_attn_lambda_k1, L0_attn_lambda_q2, L0_attn_lambda_k2, L0_attn_gamma, L0_attn_beta, L0_ffn_q_node_w, L0_ffn_q_node_b, L0_ffn_q_w1, L0_ffn_q_b1, L0_ffn_q_w2, L0_ffn_q_b2, L0_ffn_k_node_w, L0_ffn_k_node_b, L0_ffn_k_w1, L0_ffn_k_b1, L0_ffn_k_w2, L0_ffn_k_b2, L0_ffn_v_node_w, L0_ffn_v_node_b, L0_ffn_v_w1, L0_ffn_v_b1, L0_ffn_v_w2, L0_ffn_v_b2):

    def _L0_attn_ref(x, Wq, Wk, Wv, Wo, lambda_q1, lambda_k1, lambda_q2, lambda_k2, gamma, beta):
        import jax, jax.numpy as jnp
        import numpy as np
        import math
        DIM = 256
        NUM_HEADS = 16
        HEAD_DIM = DIM // NUM_HEADS
        LAYER_IDX = 12
        LAMBDA_INIT = 0.8 - 0.6 * math.exp(-0.3 * (LAYER_IDX - 1))
        LN_EPS = 1e-05
        B, S, _ = x.shape
        scaling = HEAD_DIM ** (-0.5)
        Q = (x @ Wq).reshape(B, S, NUM_HEADS, 2 * HEAD_DIM).transpose(0, 2, 1, 3)
        K = (x @ Wk).reshape(B, S, NUM_HEADS, 2 * HEAD_DIM).transpose(0, 2, 1, 3)
        V = (x @ Wv).reshape(B, S, NUM_HEADS, HEAD_DIM).transpose(0, 2, 1, 3)
        lamb = jnp.exp(jnp.sum(lambda_q1 * lambda_k1)) - jnp.exp(jnp.sum(lambda_q2 * lambda_k2)) + LAMBDA_INIT
        Q1, Q2 = jnp.split(Q, 2, axis=-1)
        K1, K2 = jnp.split(K, 2, axis=-1)
        A1 = jnp.einsum('bhqd,bhkd->bhqk', Q1, K1) * scaling
        A2 = jnp.einsum('bhqd,bhkd->bhqk', Q2, K2) * scaling
        attn = jax.nn.softmax(A1, axis=-1) - lamb * jax.nn.softmax(A2, axis=-1)
        out = jnp.einsum('bhqk,bhkd->bhqd', attn, V)
        out = out.transpose(0, 2, 1, 3).reshape(B, S, DIM)
        out = out @ Wo
        mu = jnp.mean(out, axis=-1, keepdims=True)
        var = jnp.var(out, axis=-1, keepdims=True)
        out = (out - mu) * jax.lax.rsqrt(var + LN_EPS) * gamma + beta
        return out

    def _L0_ffn_ref(x, q_node_w, q_node_b, q_w1, q_b1, q_w2, q_b2, k_node_w, k_node_b, k_w1, k_b1, k_w2, k_b2, v_node_w, v_node_b, v_w1, v_b1, v_w2, v_b2):
        import jax, jax.numpy as jnp
        import numpy as np
        LATENT = 256
        LEAF_W = 64
        DEPTH = 4
        N_LEAVES = 2 ** DEPTH
        N_NODES = 2 ** DEPTH - 1
        B, S = (4, 512)

        def _fff_params(key, prefix):
            ks = jax.random.split(key, 4)
            d, h, l, n = (LATENT, LEAF_W, N_LEAVES, N_NODES)
            s_in = 1.0 / np.sqrt(d).astype(np.float32)
            s_h = 1.0 / np.sqrt(h).astype(np.float32)
            return {f'{prefix}_node_w': jax.random.normal(ks[0], (n, d), jnp.float32) * s_in, f'{prefix}_node_b': jax.random.normal(ks[1], (n,), jnp.float32) * s_in, f'{prefix}_w1': jax.random.normal(ks[2], (l, d, h), jnp.float32) * s_in, f'{prefix}_b1': jnp.zeros((l, h), jnp.float32), f'{prefix}_w2': jax.random.normal(ks[3], (l, h, d), jnp.float32) * s_h, f'{prefix}_b2': jnp.zeros((l, d), jnp.float32)}

        def _fff(x, node_w, node_b, w1, b1, w2, b2):
            Bx, Sx, D = x.shape
            xf = x.reshape(-1, D)
            N = xf.shape[0]
            cur = jnp.zeros((N,), jnp.int32)
            for _ in range(DEPTH):
                pw = node_w[cur]
                score = jnp.einsum('nd,nd->n', xf, pw) + node_b[cur]
                cur = 2 * cur + 1 + (score >= 0).astype(jnp.int32)
            leaf = cur - N_NODES
            sel = jax.nn.one_hot(leaf, N_LEAVES, dtype=xf.dtype)
            hidden_all = jax.nn.relu(jnp.einsum('nd,ldh->lnh', xf, w1) + b1[:, None, :])
            hidden = hidden_all * sel.T[:, :, None]
            out = jnp.einsum('lnh,lho->no', hidden, w2) + sel @ b2
            return out.reshape(Bx, Sx, D)
        q = _fff(x, q_node_w, q_node_b, q_w1, q_b1, q_w2, q_b2)
        k = _fff(x, k_node_w, k_node_b, k_w1, k_b1, k_w2, k_b2)
        v = _fff(x, v_node_w, v_node_b, v_w1, v_b1, v_w2, v_b2)
        scale = 1.0 / np.sqrt(LATENT).astype(np.float32)
        attn = jax.nn.softmax(jnp.einsum('bqd,bkd->bqk', q, k) * scale, axis=-1)
        return jnp.einsum('bqk,bkd->bqd', attn, v)
    x = L0_attn_x
    xn = _layernorm(x, axis=-1)
    x = x + _L0_attn_ref(xn, L0_attn_Wq, L0_attn_Wk, L0_attn_Wv, L0_attn_Wo, L0_attn_lambda_q1, L0_attn_lambda_k1, L0_attn_lambda_q2, L0_attn_lambda_k2, L0_attn_gamma, L0_attn_beta) + _L0_ffn_ref(xn, L0_ffn_q_node_w, L0_ffn_q_node_b, L0_ffn_q_w1, L0_ffn_q_b1, L0_ffn_q_w2, L0_ffn_q_b2, L0_ffn_k_node_w, L0_ffn_k_node_b, L0_ffn_k_w1, L0_ffn_k_b1, L0_ffn_k_w2, L0_ffn_k_b2, L0_ffn_v_node_w, L0_ffn_v_node_b, L0_ffn_v_w1, L0_ffn_v_b1, L0_ffn_v_w2, L0_ffn_v_b2)
    return x

_drawn_inputs = setup_inputs


def setup_inputs(seed=0):
    import zlib

    import numpy as np

    out = dict(_drawn_inputs(seed))
    spreads = {'L0_attn_gamma': (1.0, 0.2),
     'L0_attn_beta': (0.0, 0.1),
     'L0_ffn_q_b1': (0.0, 0.8),
     'L0_ffn_q_b2': (0.0, 0.8),
     'L0_ffn_k_b1': (0.0, 0.8),
     'L0_ffn_k_b2': (0.0, 0.8),
     'L0_ffn_v_b1': (0.0, 0.8),
     'L0_ffn_v_b2': (0.0, 0.467)}
    factors = {'L0_attn_lambda_q1': 25.426,
     'L0_attn_lambda_q2': 6.203,
     'L0_attn_lambda_k2': 3.787,
     'L0_ffn_q_node_w': 6.865,
     'L0_ffn_q_node_b': 8.0,
     'L0_ffn_q_w1': 8.0,
     'L0_ffn_q_w2': 6.661,
     'L0_ffn_k_node_w': 6.736,
     'L0_ffn_k_node_b': 8.0,
     'L0_ffn_k_w1': 7.843,
     'L0_ffn_k_w2': 6.66,
     'L0_ffn_v_node_w': 2.948,
     'L0_ffn_v_node_b': 5.992,
     'L0_ffn_v_w1': 3.347}
    for name, (base, spread) in spreads.items():
        noise = np.random.default_rng([zlib.crc32(name.encode()), seed]).standard_normal(out[name].shape)
        drawn = base * np.exp(spread * noise) if base else spread * noise
        out[name] = jnp.asarray(drawn.astype(out[name].dtype))
    for name, factor in factors.items():
        out[name] = (out[name] * factor).astype(out[name].dtype)
    return out
```

```python
import math
from contextlib import ExitStack

import numpy as np

import concourse.bass as bass
from concourse import mybir

F32 = mybir.dt.float32
BF16 = mybir.dt.bfloat16
ALU = mybir.AluOpType
ACT = mybir.ActivationFunctionType
AX = mybir.AxisListType

P = 128
BATCH, SEQ, DIM = 8, 1024, 256
KC = DIM // P
TT = SEQ // P
CH = 512
NCH = SEQ // CH

NFFF, LEAVES, NODES, LEAF_W, DEPTH = 3, 16, 15, 64, 4
HID = LEAVES * LEAF_W
HT = HID // P
BIG = 2.0 ** 100

HEADS, HD = 16, 16
PARTS = 4
SETS = BATCH * HEADS // 2
TERM_Q = (0, 0, 0, 1, 1, 2)
TERM_K = (0, 1, 2, 0, 1, 0)
TERMS = len(TERM_Q)
KS = TERMS * HD
KM = KS + 3 * PARTS
RING = 4
STEPS = NCH * TT
SCALE = HD ** -0.5
LN_EPS = 1e-5
LAMBDA_INIT = 0.8 - 0.6 * math.exp(-0.3 * (12 - 1))
FFN_SCALE = 1.0 / math.sqrt(DIM)


class Arena:

    def __init__(self, base):
        self.base, self.at = base, 0

    def take(self, *shape, dt=F32):
        n = int(np.prod(shape))
        words = (n * (2 if dt == BF16 else 4) + 3) // 4
        words = (words + 7) // 8 * 8
        view = self.base[:, self.at:self.at + words]
        self.at += words
        if dt == BF16:
            view = view.bitcast(BF16)
        view = view[:, 0:n]
        if len(shape) > 1:
            names = "abcde"[:len(shape)]
            sizes = {k: v for k, v in zip(names, shape)}
            view = view.rearrange(f"p ({' '.join(names)}) -> p {' '.join(names)}", **sizes)
        return view


class Chain:

    def __init__(self, eng, sem, start=0):
        self.eng, self.sem, self.n = eng, sem, start

    def __call__(self, ins):
        ins.then_inc(self.sem, 1)
        self.n = self.n + 1
        self.eng.wait_ge(self.sem, self.n)


def rstd_newton(nc, link, out, var, guess, tmp):
    link(nc.vector.reciprocal(out, guess))
    link(nc.vector.tensor_tensor(tmp, out, out, ALU.mult))
    link(nc.vector.tensor_tensor(tmp, tmp, var, ALU.mult))
    link(nc.vector.tensor_scalar(tmp, tmp, -0.5, 1.5, ALU.mult, ALU.add))
    link(nc.vector.tensor_tensor(out, out, tmp, ALU.mult))




def ffn_stage(nc, ctx, base, ps, x, w, scratch):
    ar = Arena(base)
    xs = ar.take(TT, DIM)
    xn = ar.take(TT, DIM)
    xnT = ar.take(KC, SEQ)
    w1 = ar.take(NFFF, KC, HID)
    w2 = ar.take(NFFF, HT, DIM)
    b1 = ar.take(NFFF * HT)
    b2 = ar.take(NFFF, DIM)
    nodeT = ar.take(KC, NFFF * NODES)
    nodeb = ar.take(1)
    off_leaf = ar.take(NFFF, HT, P, dt=BF16)
    off_count = ar.take(P, dt=BF16)
    ident = ar.take(P)
    bits = ar.take(SEQ, dt=BF16)
    sel = ar.take(SEQ)
    hid = ar.take(2, HT, CH)
    qk = ar.take(2, KC, SEQ)
    v = ar.take(TT, DIM)
    prob = ar.take(2, SEQ)
    probT = ar.take(2, TT, P)
    ffn_out = ar.take(TT, DIM)
    stats = ar.take(TT, 6)
    mv = ar.take(TT, 2)
    var, guess, rstd, tmp = ar.take(TT), ar.take(TT), ar.take(TT), ar.take(TT)
    rowmax, nbias, rowsum, rinv = ar.take(2, 1), ar.take(2, 1), ar.take(2, 1), ar.take(2, 1)

    def sem(name):
        return ctx.enter_context(nc.semaphore("f_" + name))

    weights_in, x_in, xnT_out, ffn_stored = sem("weights_in"), sem("x_in"), sem("xnT_out"), sem("ffn_stored")
    var_ready, guess_ready, xn_ready = sem("var_ready"), sem("guess_ready"), sem("xn_ready")
    ring_a_full, ring_a_used = sem("ring_a_full"), sem("ring_a_used")
    ring_v_full, ring_v_used = sem("ring_v_full"), sem("ring_v_used")
    sum_in = sem("sum_in")
    nbias_ready, dchain = sem("nbias_ready"), sem("dchain")
    A_PER = 2 + 2 + NFFF * NCH * HT // 2 + 2 * TT
    V_PER = 2 + 2 + NFFF * NCH * (HT // 2 + 2) + 3 * TT
    LINKS = 5 + 1 + 3 * TT
    assert A_PER % 4 == 0 and V_PER % 4 == 0
    units = [(f, c) for f in range(NFFF) for c in range(NCH)]
    a_sel = 2
    a_hid = 4
    a_att = a_hid + len(units) * HT // 2
    v_bits = 2
    v_first = 4

    def v_hid(u):
        return v_first + u * (HT // 2) + max(u - 1, 0) * 2

    def v_out(u):
        return v_first + min(u + 2, len(units)) * (HT // 2) + u * 2

    v_att = v_first + len(units) * (HT // 2 + 2)

    def bank_a(k):
        return ps[:, (k % 4) * CH:(k % 4) * CH + CH]

    def bank_v(k):
        return ps[:, (4 + k % 4) * CH:(4 + k % 4) * CH + CH]

    def v_prob(t):
        return v_att + 3 * t

    N_W = 10
    with nc.Block() as block:

        @block.sync
        def _(sp):
            nc.sync.dma_start(xs, x[0].rearrange("(t p) d -> p t d", p=P)).then_inc(x_in, 16)
            for dst, name in ((nodeT, "nodeT"), (nodeb[0:NFFF * NODES], "nodeb"), (off_leaf, "off_leaf"),
                              (off_count, "off_count"), (ident, "ident"), (b1, "b1"), (b2, "b2")):
                nc.sync.dma_start(dst, w[name]).then_inc(weights_in, 16)
            for f in range(NFFF):
                nc.sync.dma_start(w1[:, f], w["w1"][f]).then_inc(weights_in, 16)
            nc.sync.dma_start(w2, w["w2"]).then_inc(weights_in, 16)
            with sp.Fori(0, BATCH) as b:
                sp.wait_ge(xn_ready, b + 1)
                nc.sync.dma_start(xs, x[(b + 1) % BATCH].rearrange("(t p) d -> p t d", p=P)).then_inc(x_in, 16)
                sp.wait_ge(ring_a_used, b * A_PER + 2 + 4)
                sp.wait_ge(ring_v_used, b * V_PER + 2 + 4)
                nc.sync.dma_start(scratch["xnT"][b], xnT).then_inc(xnT_out, 16)
                sp.wait_ge(ffn_stored, b * 16)
                nc.sync.dma_start(ffn_out, x[b].rearrange("(t p) d -> p t d", p=P)).then_inc(sum_in, 16)
                sp.wait_ge(ring_v_used, b * V_PER + V_PER + 4)
                nc.sync.dma_start(scratch["ffn"][b].rearrange("(t p) d -> p t d", p=P), ffn_out).then_inc(ffn_stored, 16)
            sp.wait_ge(x_in, 16 * (BATCH + 1))
            sp.wait_ge(xnT_out, 16 * BATCH)
            sp.wait_ge(ffn_stored, 16 * BATCH)

        @block.tensor
        def _(pe):
            pe.wait_ge(weights_in, 16 * (N_W + 1))
            with pe.Fori(0, BATCH) as b:
                def take_a(k):
                    pe.wait_ge(ring_a_used, b * A_PER + k + 1)
                    return bank_a(k)

                def take_v(k):
                    pe.wait_ge(ring_v_used, b * V_PER + k + 1)
                    return bank_v(k)

                pe.wait_ge(xn_ready, b + 1)
                for k in range(KC):
                    for half in range(2):
                        bank = (take_a if half else take_v)(k)
                        for q in range(4):
                            last = nc.tensor.transpose(bank[:, q * P:(q + 1) * P],
                                                       xn[:, half * 4 + q, k * P:(k + 1) * P], ident)
                        last.then_inc(ring_a_full if half else ring_v_full, 1)
                pe.wait_ge(ring_a_used, b * A_PER + 2 + 4)
                pe.wait_ge(ring_v_used, b * V_PER + 2 + 4)
                for c in range(NCH):
                    bank = take_v(v_bits + c)
                    for k in range(KC):
                        last = nc.tensor.matmul(bank[0:NFFF * NODES, :], nodeT[:, k, :],
                                                xnT[:, k, c * CH:(c + 1) * CH], start=k == 0, stop=k == KC - 1)
                    last.then_inc(ring_v_full, 1)
                for c in range(NCH):
                    pe.wait_ge(ring_v_used, b * V_PER + v_bits + c + 1 + 4)
                    nc.tensor.matmul(take_a(a_sel + c), off_count, bits[:, c * CH:(c + 1) * CH],
                                     start=True, stop=True).then_inc(ring_a_full, 1)

                def hidden(u):
                    f, c = units[u]
                    for t in range(HT):
                        odd = t % 2
                        k = t // 2 + (v_hid(u) if odd else a_hid + u * (HT // 2))
                        bank = (take_v if odd else take_a)(k)
                        cols = slice(c * CH, (c + 1) * CH)
                        nc.tensor.matmul(bank, off_leaf[:, f, t, :], bits[:, cols], start=True, stop=False)
                        for kc in range(KC):
                            last = nc.tensor.matmul(bank, w1[:, f, kc, t * P:(t + 1) * P], xnT[:, kc, cols],
                                                    start=False, stop=kc == KC - 1)
                        last.then_inc(ring_v_full if odd else ring_a_full, 1)

                def out(u):
                    f, c = units[u]
                    pe.wait_ge(ring_a_used, b * A_PER + a_hid + (u + 1) * (HT // 2) + 4)
                    pe.wait_ge(ring_v_used, b * V_PER + v_hid(u) + HT // 2 + 4)
                    for m in range(2):
                        bank = take_v(v_out(u) + m)
                        if f < 2:
                            for t in range(HT):
                                nc.tensor.matmul(bank, w2[:, f, t, m * P:(m + 1) * P], hid[:, u % 2, t, :],
                                                 start=t == 0, stop=False)
                            last = nc.tensor.matmul(bank, b2[:, f, m * P:(m + 1) * P], sel[:, c * CH:(c + 1) * CH],
                                                    start=False, stop=True)
                        else:
                            for j in range(2):
                                tok = (2 * m + j) * P
                                o = bank[:, j * DIM:(j + 1) * DIM]
                                for t in range(HT):
                                    nc.tensor.matmul(o, hid[:, u % 2, t, tok:tok + P], w2[:, f, t, :],
                                                     start=t == 0, stop=False)
                                last = nc.tensor.matmul(o, sel[:, c * CH + tok:c * CH + tok + P], b2[:, f, :],
                                                        start=False, stop=True)
                        last.then_inc(ring_v_full, 1)

                hidden(0)
                for u in range(len(units)):
                    if u + 1 < len(units):
                        hidden(u + 1)
                    out(u)

                pe.wait_ge(ring_v_used, b * V_PER + v_att + 4)

                def scores(t):
                    for c in range(NCH):
                        bank = take_a(a_att + 2 * t + c)
                        for k in range(KC):
                            last = nc.tensor.matmul(bank, qk[:, 0, k, t * P:(t + 1) * P],
                                                    qk[:, 1, k, c * CH:(c + 1) * CH], start=k == 0, stop=k == KC - 1)
                        last.then_inc(ring_a_full, 1)

                def turn(t):
                    pe.wait_ge(ring_a_used, b * A_PER + a_att + 2 * t + 2 + 4)
                    for h in range(2):
                        bank = take_v(v_prob(t) + h)
                        for q in range(4):
                            kt = 4 * h + q
                            last = nc.tensor.transpose(bank[:, q * P:(q + 1) * P],
                                                       prob[:, t % 2, kt * P:(kt + 1) * P], ident)
                        last.then_inc(ring_v_full, 1)

                def values(t):
                    pe.wait_ge(ring_v_used, b * V_PER + v_prob(t) + 2 + 4)
                    bank = take_v(v_prob(t) + 2)
                    for kt in range(TT):
                        last = nc.tensor.matmul(bank[:, 0:DIM], probT[:, t % 2, kt, :], v[:, kt, :],
                                                start=kt == 0, stop=kt == TT - 1)
                    last.then_inc(ring_v_full, 1)

                scores(0)
                for t in range(TT):
                    if t + 1 < TT:
                        scores(t + 1)
                    turn(t)
                    values(t)

        @block.scalar
        def _(act):
            act.wait_ge(var_ready, 1)
            nc.scalar.activation(guess, var, ACT.Sqrt).then_inc(guess_ready, 1)
            act.wait_ge(weights_in, 16 * (N_W + 1))
            with act.Fori(0, BATCH) as b:
                def full(k):
                    act.wait_ge(ring_a_full, b * A_PER + k + 1)
                    return bank_a(k)

                act.wait_ge(xnT_out, b * 16)
                for k in range(KC):
                    nc.scalar.activation(xnT[:, k, CH:SEQ], full(k), ACT.Copy).then_inc(ring_a_used, 1)
                for c in range(NCH):
                    nc.scalar.activation(sel[:, c * CH:(c + 1) * CH], full(a_sel + c), ACT.Relu,
                                         scale=-1.0, bias=1.0).then_inc(ring_a_used, 1)
                for u, (f, c) in enumerate(units):
                    for t in range(0, HT, 2):
                        nc.scalar.activation(hid[:, u % 2, t, :], full(a_hid + u * (HT // 2) + t // 2), ACT.Relu,
                                             bias=b1[:, f * HT + t:f * HT + t + 1]).then_inc(ring_a_used, 1)
                act.wait_ge(var_ready, b + 2)
                nc.scalar.activation(guess, var, ACT.Sqrt).then_inc(guess_ready, 1)
                for t in range(TT):
                    full(a_att + 2 * t + 1)
                    act.wait_ge(nbias_ready, b * TT + t + 1)
                    if t >= 2:
                        act.wait_ge(ring_v_used, b * V_PER + v_prob(t - 2) + 3 + 4)
                    bk = (a_att + 2 * t) % 4 * CH
                    nc.scalar.activation(prob[:, t % 2, :], ps[:, bk:bk + SEQ], ACT.Exp, scale=FFN_SCALE,
                                         bias=nbias[:, t % 2], accum_out=rowsum[:, t % 2]).then_inc(ring_a_used, 2)

        @block.vector
        def _(dve):
            link0 = Chain(dve, dchain)

            def norm_stats(link, bb):
                dve.wait_ge(x_in, bb * 16 + 16)
                for t in range(TT):
                    ins = nc.vector.bn_stats(stats[:, t, :], xs[:, t, :])
                link(ins)
                nc.vector.memset(tmp, 0.0)
                for t in range(TT):
                    ins = nc.vector.bn_aggr(mv[:, t, :], stats[:, t, :])
                link(ins)
                nc.vector.tensor_scalar(var, mv[:, :, 1], LN_EPS, None, ALU.add).then_inc(var_ready, 1)

            def norm_apply(link, bb):
                dve.wait_ge(guess_ready, bb + 1)
                rstd_newton(nc, link, rstd, var, guess, tmp)
                for t in range(TT):
                    ins = nc.vector.tensor_scalar(xn[:, t, :], xs[:, t, :], mv[:, t, 0:1], rstd[:, t:t + 1],
                                                  ALU.subtract, ALU.mult)
                ins.then_inc(xn_ready, 1)

            link0(nc.vector.memset(bits, 1.0))
            nc.vector.memset(rowsum, 0.0).then_inc(ring_a_used, 4)
            nc.vector.memset(rowmax, 0.0).then_inc(ring_v_used, 4)
            norm_stats(link0, 0)
            norm_apply(link0, 0)
            n0 = link0.n
            dve.wait_ge(weights_in, 16 * (N_W + 1))
            per_batch = 2 + 5 + TT * 2

            with dve.Fori(0, BATCH) as b:
                link = Chain(dve, dchain, b * per_batch + n0)

                def full(k):
                    dve.wait_ge(ring_v_full, b * V_PER + k + 1)
                    return bank_v(k)

                dve.wait_ge(xnT_out, b * 16)
                for k in range(KC):
                    nc.vector.tensor_copy(xnT[:, k, 0:CH], full(k)).then_inc(ring_v_used, 1)
                for c in range(NCH):
                    nc.vector.tensor_scalar(bits[0:NFFF * NODES, c * CH:(c + 1) * CH],
                                            full(v_bits + c)[0:NFFF * NODES, :], nodeb[0:NFFF * NODES], 0.0,
                                            ALU.add, ALU.is_ge).then_inc(ring_v_used, 1)

                def hidden(u):
                    f, c = units[u]
                    for t in range(1, HT, 2):
                        nc.vector.tensor_scalar(hid[:, u % 2, t, :], full(v_hid(u) + t // 2),
                                                b1[:, f * HT + t:f * HT + t + 1], 0.0, ALU.add, ALU.max
                                                ).then_inc(ring_v_used, 1)

                def out(u):
                    f, c = units[u]
                    for m in range(2):
                        src = full(v_out(u) + m)
                        if f < 2:
                            dst = qk[:, f, m, c * CH:(c + 1) * CH]
                        else:
                            dst = v[:, 4 * c + 2 * m:4 * c + 2 * m + 2, :].rearrange("p t d -> p (t d)")
                        nc.vector.tensor_copy(dst, src).then_inc(ring_v_used, 1)

                hidden(0)
                for u in range(len(units)):
                    if u + 1 < len(units):
                        hidden(u + 1)
                    out(u)
                    if u == 2:
                        norm_stats(link, b + 1)

                def row_max(t):
                    dve.wait_ge(ring_a_full, b * A_PER + a_att + 2 * t + 2)
                    bk = (a_att + 2 * t) % 4 * CH
                    link(nc.vector.tensor_reduce(rowmax[:, t % 2], ps[:, bk:bk + SEQ], AX.X, ALU.max))
                    nc.vector.tensor_scalar(nbias[:, t % 2], rowmax[:, t % 2], -FFN_SCALE, None, ALU.mult
                                            ).then_inc(nbias_ready, 1)

                row_max(0)
                dve.wait_ge(sum_in, b * 16 + 16)
                for t in range(TT):
                    if t + 1 < TT:
                        row_max(t + 1)
                    for h in range(2):
                        nc.vector.tensor_copy(probT[:, t % 2, 4 * h:4 * h + 4, :].rearrange("p a b -> p (a b)"),
                                              full(v_prob(t) + h)).then_inc(ring_v_used, 1)
                    link(nc.vector.reciprocal(rinv[:, t % 2], rowsum[:, t % 2]))
                    nc.vector.scalar_tensor_tensor(ffn_out[:, t, :], full(v_prob(t) + 2)[:, 0:DIM], rinv[:, t % 2],
                                                   ffn_out[:, t, :], ALU.mult, ALU.add).then_inc(ring_v_used, 1)
                    if t == 3:
                        norm_apply(link, b + 1)




def attention_stage(nc, ctx, base, ps, w, scratch):
    ar = Arena(base)
    ring = ar.take(RING, 2, PARTS, SEQ, dt=BF16)
    split = ar.take(2, 3, SEQ, dt=BF16)
    rest = ar.take(2, SEQ)
    xnT = ar.take(KC, SEQ)
    wqk = ar.take(KC, 2, P)
    wv = ar.take(KC, PARTS * HD)
    vaug = ar.take(2, TT, 4, 32)
    prob = ar.take(2, PARTS, CH)
    osb = ar.take(NCH, CH)
    ident = ar.take(P)
    identb = ar.take(P, dt=BF16)
    omul = ar.take(4, PARTS, HD)
    linv = ar.take(4, PARTS)
    oset = ar.take(TT, P)
    halfmax = ar.take(PARTS, TT, NCH)
    smax = ar.take(PARTS, TT)
    mrest = ar.take(PARTS, TT)
    mparts = ar.take(TT, PARTS, 3, dt=BF16)
    mrow = ar.take(SEQ, dt=BF16)
    zeros = ar.take(SEQ, dt=BF16)
    lam_in = ar.take(4, HD)
    lam_prod = ar.take(HD)
    lam_dot, lam_exp, lam = ar.take(2), ar.take(2), ar.take(1)
    sign = ar.take(4, PARTS)

    def sem(name):
        return ctx.enter_context(nc.semaphore("a_" + name))

    consts_in, lam_loaded = sem("consts_in"), sem("lam_loaded")
    tile_in = sem("tile_in")
    split_stored = sem("split_stored")
    slot_in = [sem(f"slot{s}_in") for s in range(RING)]
    oset_stored = sem("oset_stored")
    lam_dots, lam_exps = sem("lam_dots"), sem("lam_exps")
    aux_full, aux_used = sem("aux_full"), sem("aux_used")
    score_full, exp_done = sem("score_full"), sem("exp_done")
    value_done, value_copied, oturned = sem("value_done"), sem("value_copied"), sem("oturned")
    split_ready, oset_ready = sem("split_ready"), sem("oset_ready")
    mparts_ready, shift_ready = sem("mparts_ready"), sem("shift_ready")
    zeros_ready = sem("zeros_ready")
    dchain, pchain = sem("dchain"), sem("pchain")

    score = ps[:, 0:4 * CH].rearrange("p (a b) -> p a b", a=PARTS)
    value_bank = ps[:, 4 * CH:5 * CH]
    AUX = 3
    aux_bank = [ps[:, (5 + n) * CH:(6 + n) * CH] for n in range(AUX)]
    aux_bf16 = [a.bitcast(BF16) for a in aux_bank]
    ITERS = SETS // RING
    SCORES = 2 * STEPS * RING

    V_TILES = ((0, 3), (3, 6), (6, 8))

    def extras(s, step, tail):
        out = []
        if step == 1 and s % 2 == 0 and not (tail and s == 2):
            out += [("v", n) for n in range(len(V_TILES))]
        if step in (1, 2, 3, 4) and s % 2 == 1 and not tail:
            out.append(("qk", step - 1))
        if step == 2 and not (tail and s == 3):
            out.append(("shift", 0))
        if step == 4 and s > 0:
            out.append(("o", 1))
        if step == 11:
            out.append(("o", 0))
        if not (tail and s >= 2):
            out += [("max", 4 * step + n) for n in range(4)]
        if s == RING - 1 and step == STEPS - 1:
            out.append(("o", 2))
        return out

    def uses_before(s, step, kind, number, tail=False):
        count = 0
        for s2 in range(RING):
            for step2 in range(STEPS):
                for one in extras(s2, step2, tail):
                    count += 1
                    if (s2, step2, one) == (s, step, (kind, number)):
                        return count
        return count

    MAXIMA = PARTS * TT * NCH
    PROLOGUE = [("qk", 0, n) for n in range(4)] + [("v", 0, n) for n in range(len(V_TILES))] + [("qk", 1, n) for n in range(4)] + \
        [("max", 0, n) for n in range(MAXIMA)] + [("shift", 0, 0)] + [("max", 1, n) for n in range(MAXIMA)]
    PRO = len(PROLOGUE)
    PER_ITER = uses_before(RING, 0, "", 0)
    LAST_V = len(V_TILES) - 1
    assert PER_ITER % AUX == 0

    with nc.Block() as block:

        @block.sync
        def _(sp):
            nc.sync.dma_start(ident, w["ident"]).then_inc(consts_in, 16)
            nc.sync.dma_start(identb, w["identb"]).then_inc(consts_in, 16)
            for s in range(RING):
                nc.sync.dma_start(ring[KS:KM, s, 1], w["pick"]).then_inc(consts_in, 16)
            for n, name in enumerate(("lq1", "lk1", "lq2", "lk2")):
                nc.sync.dma_start(lam_in[:, n], w[name].partition_broadcast(P)).then_inc(lam_loaded, 16)

            def load_tile(t):
                nc.sync.dma_start(xnT, scratch["xnT"][t // 4]).then_inc(tile_in, 16)
                nc.sync.dma_start(wqk, w["wqk"][t % 4]).then_inc(tile_in, 16)
                nc.sync.dma_start(wv, w["wv"][t % 4]).then_inc(tile_in, 16)

            def store_split(t):
                sp.wait_ge(split_ready, t * 4 + 4)
                for a in range(2):
                    nc.sync.dma_start(scratch["split"][t, a].rearrange("s p t -> p s t"), split[:, a]
                                      ).then_inc(split_stored, 16)
                sp.wait_ge(split_stored, t * 32 + 32)

            def load_set(t, half, slot):
                for a, parts in enumerate((TERM_Q, TERM_K)):
                    for i, part in enumerate(parts):
                        src = scratch["split"][t, a, part, 64 * half:64 * half + 64, :]
                        nc.sync.dma_start(ring[HD * i:HD * (i + 1), slot, a],
                                          src.rearrange("(j d) t -> d j t", d=HD)).then_inc(slot_in[slot], 16)

            load_tile(0)
            store_split(0)
            load_set(0, 0, 0)
            load_set(0, 1, 1)
            sp.wait_ge(aux_used, PROLOGUE.index(("v", 0, LAST_V)) + 1 + AUX)
            load_tile(1)
            store_split(1)
            load_set(1, 0, 2)

            def body(i, tail):
                for s in range(RING):
                    sp.wait_ge(score_full, i * SCORES + 2 * STEPS * s)
                    if s % 2 == 0:
                        if not (tail and s == 2):
                            load_set(i * 2 + (s // 2 + 1), 1, (s + 3) % RING)
                        if not tail:
                            sp.wait_ge(aux_used, i * PER_ITER + (PRO + AUX + uses_before(s, 1, "v", LAST_V)))
                            load_tile(i * 2 + (s // 2 + 2))
                    elif not tail:
                        store_split(i * 2 + (s // 2 + 2))
                        load_set(i * 2 + (s // 2 + 2), 0, (s + 3) % RING)
                sp.wait_ge(oset_ready, i * (2 * RING) + (2 * RING + 2))
                nc.sync.dma_start(scratch["o"][i].rearrange("t p d -> p t d"), oset).then_inc(oset_stored, 16)

            with sp.Fori(0, ITERS - 1) as i:
                body(i, False)
            body(ITERS - 1, True)
            sp.wait_ge(oset_stored, 16 * ITERS)

        @block.tensor
        def _(pe):
            def aux(k):
                pe.wait_ge(aux_used, k + 1)

            def project_qk(t, number, bank):
                a, c = number // 2, number % 2
                pe.wait_ge(tile_in, t * 48 + 48)
                for kc in range(KC):
                    last = nc.tensor.matmul(aux_bank[bank], wqk[:, kc, a, :], xnT[:, kc, c * CH:(c + 1) * CH],
                                            start=kc == 0, stop=kc == KC - 1)
                last.then_inc(aux_full, 1)

            def project_v(number, bank):
                first, end = V_TILES[number]
                for tt in range(first, end):
                    for kc in range(KC):
                        last = nc.tensor.matmul(aux_bank[bank][:, (tt - first) * 64:(tt - first + 1) * 64],
                                                xnT[:, kc, tt * P:(tt + 1) * P], wv[:, kc, :],
                                                start=kc == 0, stop=kc == KC - 1)
                last.then_inc(aux_full, 1)

            def row_scores(number, slot, bank):
                j, qt, c = number // (TT * NCH), number // NCH % TT, number % NCH
                nc.tensor.matmul(aux_bank[bank], ring[0:KS, slot, 0, j, qt * P:(qt + 1) * P],
                                 ring[0:KS, slot, 1, j, c * CH:(c + 1) * CH], start=True, stop=True
                                 ).then_inc(aux_full, 1)

            def turn_shift(n, bank):
                pe.wait_ge(mparts_ready, n + 1)
                for qt in range(TT):
                    last = nc.tensor.transpose(aux_bf16[bank][KS:KM, qt * P:(qt + 1) * P],
                                               mparts[:, qt].rearrange("p a b -> p (a b)"), identb,
                                               tile_position=(0, KS))
                last.then_inc(aux_full, 1)

            def turn_o(c, n, bank):
                pe.wait_ge(value_copied, n * 2 + (c + 1 + 2))
                for q in range(4):
                    last = nc.tensor.transpose(aux_bank[bank][:, q * P:(q + 1) * P], osb[:, c, q * P:(q + 1) * P],
                                               ident)
                last.then_inc(aux_full, 1)

            def scores(i, s, step, h):
                c, kt = step // TT, step % TT
                g = 2 * (STEPS * s + step)
                if step == 0 and h == 0:
                    pe.wait_ge(shift_ready, i * RING + (s + 1))
                pe.wait_ge(exp_done, i * SCORES + (g + h + 1))
                for j in (2 * h, 2 * h + 1):
                    last = nc.tensor.matmul(score[:, j, :], ring[0:KM, s, 1, j, kt * P:(kt + 1) * P],
                                            ring[0:KM, s, 0, j, c * CH:(c + 1) * CH], start=True, stop=True)
                last.then_inc(score_full, 1)

            def values(i, s, step):
                c, kt = step // TT, step % TT
                pe.wait_ge(exp_done, i * SCORES + (2 * (STEPS * s + step) + 2 + 2))
                if kt == 0:
                    pe.wait_ge(value_copied, i * (2 * RING) + (2 * s + c + 2))
                for j in range(PARTS):
                    last = nc.tensor.matmul(value_bank[32 * j:32 * j + 32, :],
                                            vaug[:, s // 2, kt, 2 * (s % 2) + j // 2, :], prob[:, step % 2, j, :],
                                            start=kt == 0, stop=kt == TT - 1, tile_position=(0, 32 * j))
                last.then_inc(value_done, 1)

            pe.wait_ge(consts_in, 16 * (2 + RING))
            for k, (kind, n, number) in enumerate(PROLOGUE):
                aux(k)
                if kind == "qk":
                    project_qk(n, number, k % AUX)
                elif kind == "v":
                    project_v(number, k % AUX)
                elif kind == "shift":
                    turn_shift(n, k % AUX)
                else:
                    if number == 0:
                        pe.wait_ge(slot_in[n], 12 * 16)
                    row_scores(number, n, k % AUX)

            def body(i, tail):
                k = 0
                for s in range(RING):
                    for step in range(STEPS):
                        todo = extras(s, step, tail)
                        scores_at, values_at = len(todo) // 4, len(todo) // 2
                        scores(i, s, step, 0)
                        for n, (kind, number) in enumerate(todo + [("", 0)]):
                            if n == scores_at:
                                scores(i, s, step, 1)
                            if n == values_at:
                                if step > 0:
                                    values(i, s, step - 1)
                                elif s > 0:
                                    values(i, s - 1, STEPS - 1)
                            if kind == "":
                                break
                            if (kind, number) == ("o", 2):
                                values(i, s, step)
                            aux(i * PER_ITER + (PRO + k))
                            bank = (PRO + k) % AUX
                            k += 1
                            if kind == "v":
                                project_v(number, bank)
                            elif kind == "qk":
                                project_qk(i * 2 + (s // 2 + 2), number, bank)
                            elif kind == "shift":
                                turn_shift(i * RING + (s + 1), bank)
                            elif kind == "o":
                                turn_o(0 if number == 0 else 1, i * RING + (s - 1 if number == 1 else s), bank)
                            else:
                                if number == 0:
                                    pe.wait_ge(slot_in[(s + 2) % RING], i * 192 + 192 * (1 + (s + 2) // RING))
                                row_scores(number, (s + 2) % RING, bank)

            with pe.Fori(0, ITERS - 1) as i:
                body(i, False)
            body(ITERS - 1, True)

        @block.scalar
        def _(act):
            act.wait_ge(lam_dots, 1)
            nc.scalar.activation(lam_exp, lam_dot, ACT.Exp).then_inc(lam_exps, 1)

            def copy_values(i, s, c):
                act.wait_ge(value_done, i * (STEPS * RING) + (STEPS * s + TT * (c + 1) + 2))
                act.wait_ge(oset_ready, i * (2 * RING) + (2 * s + c + 1))
                nc.scalar.activation(osb[:, c, :], value_bank, ACT.Copy).then_inc(value_copied, 1)

            def body(i):
                for s in range(RING):
                    for step in range(STEPS):
                        g = STEPS * s + step
                        act.wait_ge(value_done, i * (STEPS * RING) + (g + 1))
                        for h in range(2):
                            act.wait_ge(score_full, i * SCORES + (2 * g + h + 1))
                            nc.scalar.activation(prob[:, step % 2, 2 * h:2 * h + 2, :], score[:, 2 * h:2 * h + 2, :],
                                                 ACT.Exp, scale=SCALE).then_inc(exp_done, 1)
                        if step == TT:
                            copy_values(i, s, 0)
                        if step == 0 and s > 0:
                            copy_values(i, s - 1, 1)
                copy_values(i, RING - 1, 1)

            with act.Fori(0, ITERS) as i:
                body(i)

        @block.gpsimd
        def _(pool):
            def split_rest(t, used):
                for number in range(4):
                    a, c = number // 2, number % 2
                    cols = slice(c * CH, (c + 1) * CH)
                    pool.wait_ge(aux_used, used(number))
                    nc.gpsimd.tensor_tensor(split[:, a, 1, cols], rest[:, a, cols], zeros[:, 0:CH], ALU.add
                                            ).then_inc(pchain, 1)
                    pool.wait_ge(pchain, t * 4 + (number + 1))
                    nc.gpsimd.tensor_tensor(split[:, a, 2, cols], rest[:, a, cols], split[:, a, 1, cols],
                                            ALU.subtract).then_inc(split_ready, 1)

            def place_shift(slot, used, splits):
                pool.wait_ge(split_ready, splits)
                pool.wait_ge(aux_used, used)
                for j in range(PARTS):
                    last = nc.gpsimd.tensor_tensor(ring[KS:KM, slot, 0, j, :], mrow[KS:KM, :], zeros[KS:KM, :], ALU.add)
                last.then_inc(shift_ready, 1)

            pool.wait_ge(zeros_ready, 1)
            for t in range(2):
                split_rest(t, lambda number: PROLOGUE.index(("qk", t, number)) + 1 + AUX)
            place_shift(0, PROLOGUE.index(("shift", 0, 0)) + 1 + AUX, 8)

            def body(i, tail):
                def used(s, step, kind, number):
                    return i * PER_ITER + (PRO + AUX + uses_before(s, step, kind, number, tail))

                for s in range(RING):
                    if not (tail and s == RING - 1):
                        place_shift((s + 1) % RING, used(s, 2, "shift", 0),
                                    ITERS * 8 if tail else i * 8 + (8 + s // 2 * 4))
                    if s % 2 == 1 and not tail:
                        pool.wait_ge(shift_ready, i * RING + (s + 2))
                        split_rest(i * 2 + (s // 2 + 2), lambda number: used(s, 1 + number, "qk", number))

            with pool.Fori(0, ITERS - 1) as i:
                body(i, False)
            body(ITERS - 1, True)

        @block.vector
        def _(dve):
            link = Chain(dve, dchain)
            nc.vector.memset(lam[:, 0:1], 0.0).then_inc(aux_used, AUX)
            nc.vector.memset(sign[:, :, 0], 1.0).then_inc(exp_done, 2)
            nc.vector.memset(sign[:, :, 2], 1.0).then_inc(value_done, 2)
            nc.vector.memset(linv, 0.0).then_inc(value_copied, 2)
            nc.vector.memset(omul, 0.0).then_inc(oset_ready, 2)
            nc.vector.memset(zeros, 0.0).then_inc(zeros_ready, 1)
            link(nc.vector.memset(vaug, 0.0))
            nc.vector.memset(vaug[:, 0, :, :, HD:HD + 1], 1.0)
            link(nc.vector.memset(vaug[:, 1, :, :, HD:HD + 1], 1.0))
            dve.wait_ge(lam_loaded, 64)
            for n in range(2):
                link(nc.vector.tensor_tensor(lam_prod, lam_in[:, 2 * n], lam_in[:, 2 * n + 1], ALU.mult))
                ins = nc.vector.tensor_reduce(lam_dot[:, n:n + 1], lam_prod, AX.X, ALU.add)
                if n == 0:
                    link(ins)
            ins.then_inc(lam_dots, 1)
            dve.wait_ge(lam_exps, 1)
            link(nc.vector.tensor_tensor(lam, lam_exp[:, 0:1], lam_exp[:, 1:2], ALU.subtract))
            link(nc.vector.tensor_scalar(lam, lam, LAMBDA_INIT, -1.0, ALU.add, ALU.mult))
            for j in (1, 3):
                link(nc.vector.tensor_scalar(sign[:, :, j], linv[:, :, 0], lam, None, ALU.add))

            def full(k):
                dve.wait_ge(aux_full, k + 1)

            def read_qk(link, t, number, bank):
                a, c = number // 2, number % 2
                cols = slice(c * CH, (c + 1) * CH)
                if number == 0:
                    dve.wait_ge(split_stored, t * 32)
                link(nc.vector.tensor_copy(split[:, a, 0, cols], aux_bank[bank]))
                nc.vector.tensor_tensor(rest[:, a, cols], aux_bank[bank], split[:, a, 0, cols], ALU.subtract
                                        ).then_inc(aux_used, 1)

            def read_v(number, slot, bank):
                first, end = V_TILES[number]
                src = aux_bank[bank][:, 0:(end - first) * 64].rearrange("p (t h d) -> p t h d", t=end - first, h=4)
                nc.vector.tensor_copy(vaug[:, slot, first:end, :, 0:HD], src).then_inc(aux_used, 1)

            def read_max(link, number, bank):
                j, qt, c = number // (TT * NCH), number // NCH % TT, number % NCH
                nc.vector.tensor_reduce(halfmax[:, j, qt, c:c + 1], aux_bank[bank], AX.X, ALU.max
                                        ).then_inc(aux_used, 1)

            def split_max(link, uses):
                dve.wait_ge(aux_used, uses)
                link(nc.vector.tensor_reduce(smax, halfmax, AX.X, ALU.max))
                neg = mparts.rearrange("p t j s -> p s j t")
                link(nc.vector.tensor_scalar(neg[:, 0], smax, -1.0, None, ALU.mult))
                link(nc.vector.scalar_tensor_tensor(mrest, smax, -1.0, neg[:, 0], ALU.mult, ALU.subtract))
                link(nc.vector.tensor_copy(neg[:, 1], mrest))
                nc.vector.tensor_tensor(neg[:, 2], mrest, neg[:, 1], ALU.subtract).then_inc(mparts_ready, 1)

            def read_shift(n, bank):
                dve.wait_ge(shift_ready, n)
                nc.vector.tensor_copy(mrow[KS:KM, :], aux_bf16[bank][KS:KM, :]).then_inc(aux_used, 1)

            def read_o(link, i, s, c, k, bank):
                src = aux_bank[bank].rearrange("p (q j d) -> p q j d", q=4, j=PARTS)
                link(nc.vector.reciprocal(linv, src[:, :, :, HD]))
                link(nc.vector.tensor_tensor(linv, linv, sign, ALU.mult))
                nc.vector.tensor_tensor(omul, src[:, :, :, 0:HD], linv.unsqueeze(3).to_broadcast([P, 4, PARTS, HD]),
                                        ALU.mult).then_inc(aux_used, 1)
                dve.wait_ge(aux_used, k + 1 + AUX)
                if s == 0 and c == 0:
                    dve.wait_ge(oset_stored, i * 16)
                maps = omul.rearrange("p q (h m) d -> p q h m d", m=2)
                dst = oset[:, 4 * c:4 * c + 4, 32 * s:32 * s + 32].rearrange("p q (h d) -> p q h d", h=2)
                nc.vector.tensor_tensor(dst, maps[:, :, :, 0], maps[:, :, :, 1], ALU.add).then_inc(oset_ready, 1)

            for k, (kind, n, number) in enumerate(PROLOGUE):
                full(k)
                if kind == "qk":
                    read_qk(link, n, number, k % AUX)
                elif kind == "v":
                    read_v(number, n, k % AUX)
                elif kind == "shift":
                    read_shift(n, k % AUX)
                else:
                    read_max(link, number, k % AUX)
                    if number == MAXIMA - 1:
                        split_max(link, k + 1 + AUX)
            links_before = link.n

            def links_in(tail):
                kinds = [e for s in range(RING) for step in range(STEPS) for e in extras(s, step, tail)]
                return sum({"qk": 1, "o": 2}.get(kind, 0) for kind, _ in kinds) + \
                    4 * sum(e == ("max", MAXIMA - 1) for e in kinds)

            per_iter = links_in(False)

            def body(i, tail):
                link = Chain(dve, dchain, i * per_iter + links_before)
                k = 0
                for s in range(RING):
                    for step in range(STEPS):
                        for kind, number in extras(s, step, tail):
                            at = i * PER_ITER + (PRO + k)
                            full(at)
                            bank = (PRO + k) % AUX
                            k += 1
                            if kind == "v":
                                read_v(number, (s // 2 + 1) % 2, bank)
                            elif kind == "qk":
                                read_qk(link, i * 2 + (s // 2 + 2), number, bank)
                            elif kind == "shift":
                                read_shift(i * RING + (s + 1), bank)
                            elif kind == "o":
                                read_o(link, i, s - 1 if number == 1 else s, 0 if number == 0 else 1, at, bank)
                            else:
                                read_max(link, number, bank)
                                if number == MAXIMA - 1:
                                    split_max(link, at + 1 + AUX)

            with dve.Fori(0, ITERS - 1) as i:
                body(i, False)
            body(ITERS - 1, True)




def output_stage(nc, ctx, base, ps, w, scratch, out):
    ar = Arena(base)
    G = 4
    o_in = ar.take(2, 2, G, P)
    f_in = ar.take(2, G, DIM)
    oT = ar.take(2, G, KC, P)
    y = ar.take(2, G, DIM)
    wo = ar.take(KC, DIM)
    gamma = ar.take(DIM)
    beta = ar.take(DIM)
    ident = ar.take(P)
    stats = ar.take(G, 6)
    mv = ar.take(G, 2)
    var, guess, rstd, tmp = ar.take(G), ar.take(G), ar.take(G), ar.take(G)

    def sem(name):
        return ctx.enter_context(nc.semaphore("o_" + name))

    consts_in = sem("consts_in")
    group_in = [sem(f"group{h}_in") for h in range(2)]
    stored = [sem(f"stored{h}") for h in range(2)]
    turned, turned_copied, projected = sem("turned"), sem("turned_copied"), sem("projected")
    var_ready, guess_ready, rest_ready, y_ready = sem("var_ready"), sem("guess_ready"), sem("rest_ready"), sem("y_ready")
    dchain = sem("dchain")

    def turn_bank(h, n):
        return ps[:, (4 * h + n) * CH:(4 * h + n + 1) * CH]

    def out_tile(h, q):
        at = (4 * h + 2) * CH + q * DIM
        return ps[:, at:at + DIM]

    def tokens(a, b, h):
        return a[b, h * G * P:(h + 1) * G * P, :].rearrange("(t p) d -> p t d", p=P)

    with nc.Block() as block:

        @block.sync
        def _(sp):
            nc.sync.dma_start(wo, w["wo"]).then_inc(consts_in, 16)
            nc.sync.dma_start(ident, w["ident"]).then_inc(consts_in, 16)
            nc.sync.dma_start(gamma, w["gamma"].partition_broadcast(P)).then_inc(consts_in, 16)
            nc.sync.dma_start(beta, w["beta"].partition_broadcast(P)).then_inc(consts_in, 16)

            def load(b, h):
                for half in range(2):
                    src = scratch["o"][b * 2 + half, G * h:G * h + G]
                    nc.sync.dma_start(o_in[:, h, half], src.rearrange("t p d -> p t d")).then_inc(group_in[h], 16)
                nc.sync.dma_start(f_in[:, h], tokens(scratch["ffn"], b, h)).then_inc(group_in[h], 16)

            load(0, 0)
            load(0, 1)
            with sp.Fori(0, BATCH) as b:
                for h in range(2):
                    sp.wait_ge(y_ready, b * 2 + (h + 1))
                    nc.sync.dma_start(tokens(out, b, h), y[:, h]).then_inc(stored[h], 16)
                    load((b + 1) % BATCH, h)
            for h in range(2):
                sp.wait_ge(stored[h], 16 * BATCH)
                sp.wait_ge(group_in[h], 48 * (BATCH + 1))

        @block.tensor
        def _(pe):
            pe.wait_ge(consts_in, 64)
            with pe.Fori(0, BATCH) as b:
                for h in range(2):
                    pe.wait_ge(group_in[h], b * 48 + 48)
                    for n in range(2):
                        for q2 in range(2):
                            for kc in range(KC):
                                at = (q2 * KC + kc) * P
                                last = nc.tensor.transpose(turn_bank(h, n)[:, at:at + P],
                                                           o_in[:, h, kc, 2 * n + q2], ident)
                        last.then_inc(turned, 1)
                    pe.wait_ge(y_ready, b * 2 + h)
                    for q in range(G):
                        if q % 2 == 0:
                            pe.wait_ge(turned_copied, b * 4 + (2 * h + q // 2 + 1))
                        for kc in range(KC):
                            last = nc.tensor.matmul(out_tile(h, q), oT[:, h, q, kc], wo[:, kc], start=kc == 0,
                                                    stop=kc == KC - 1)
                        if q % 2 == 1:
                            last.then_inc(projected, 1)

        @block.scalar
        def _(act):
            with act.Fori(0, BATCH) as b:
                for h in range(2):
                    for n in range(2):
                        act.wait_ge(turned, b * 4 + (2 * h + n + 1))
                        nc.scalar.activation(oT[:, h, 2 * n:2 * n + 2], turn_bank(h, n), ACT.Copy
                                             ).then_inc(turned_copied, 1)
                    act.wait_ge(var_ready, b * 2 + (h + 1))
                    nc.scalar.activation(guess, var, ACT.Sqrt).then_inc(guess_ready, 1)

        @block.gpsimd
        def _(pool):
            pool.wait_ge(consts_in, 64)
            with pool.Fori(0, BATCH) as b:
                for h in range(2):
                    pool.wait_ge(group_in[h], b * 48 + 48)
                    nc.gpsimd.tensor_tensor(f_in[:, h], f_in[:, h], beta.unsqueeze(1).to_broadcast([P, G, DIM]),
                                            ALU.add).then_inc(rest_ready, 1)

        @block.vector
        def _(dve):
            dve.wait_ge(consts_in, 64)
            per_batch = 2 * (2 + 5 + 2)
            with dve.Fori(0, BATCH) as b:
                link = Chain(dve, dchain, b * per_batch)
                for h in range(2):
                    for q in range(G):
                        dve.wait_ge(projected, b * 4 + (2 * h + q // 2 + 1))
                        ins = nc.vector.bn_stats(stats[:, q], out_tile(h, q))
                    link(ins)
                    nc.vector.memset(tmp, 0.0)
                    for q in range(G):
                        ins = nc.vector.bn_aggr(mv[:, q], stats[:, q])
                    link(ins)
                    nc.vector.tensor_scalar(var, mv[:, :, 1], LN_EPS, None, ALU.add).then_inc(var_ready, 1)
                    dve.wait_ge(guess_ready, b * 2 + (h + 1))
                    rstd_newton(nc, link, rstd, var, guess, tmp)
                    dve.wait_ge(stored[h], b * 16)
                    for q in range(G):
                        ins = nc.vector.tensor_scalar(y[:, h, q], out_tile(h, q), mv[:, q, 0:1], rstd[:, q:q + 1],
                                                      ALU.subtract, ALU.mult)
                    link(ins)
                    link(nc.vector.tensor_tensor(y[:, h], y[:, h], gamma.unsqueeze(1).to_broadcast([P, G, DIM]),
                                                 ALU.mult))
                    dve.wait_ge(rest_ready, b * 2 + (h + 1))
                    nc.vector.tensor_tensor(y[:, h], y[:, h], f_in[:, h], ALU.add).then_inc(y_ready, 1)




def leaf_path(leaf):
    cur, path = 0, []
    for depth in range(DEPTH - 1, -1, -1):
        side = leaf >> depth & 1
        path.append((cur, side))
        cur = 2 * cur + 1 + side
    return path


def tree_constants():
    count = np.zeros((P, P), np.float32)
    one = NFFF * NODES
    for f in range(NFFF):
        for leaf in range(LEAVES):
            for node, side in leaf_path(leaf):
                count[f * NODES + node, f * LEAVES + leaf] += -1.0 if side else 1.0
                if side:
                    count[one, f * LEAVES + leaf] += 1.0
    unit = np.repeat(count[:, :NFFF * LEAVES], LEAF_W, axis=1) * -BIG
    return count, unit.reshape(P, NFFF, HT, P)


def build(nc, args):
    with ExitStack() as ctx:
        scratch = {
            "xnT": nc.dram_tensor("scratch_xnT", [BATCH, P, KC, SEQ], F32, kind="Internal").ap(),
            "ffn": nc.dram_tensor("scratch_ffn", [BATCH, SEQ, DIM], F32, kind="Internal").ap(),
            "split": nc.dram_tensor("scratch_split", [SETS // 2, 2, 3, P, SEQ], BF16, kind="Internal").ap(),
            "o": nc.dram_tensor("scratch_o", [SETS // RING, TT, P, P], F32, kind="Internal").ap(),
        }
        base = ctx.enter_context(nc.sbuf_tensor("arena", [P, 52800], F32))
        ps = ctx.enter_context(nc.psum_tensor("psum", [P, 8 * CH], F32))
        ffn_stage(nc, ctx, base, ps, args["x"], args, scratch)
        attention_stage(nc, ctx, base, ps, args, scratch)
        output_stage(nc, ctx, base, ps, args, scratch, args["out"])


def laid_out(inputs):
    bf16 = mybir.dt.np(BF16)
    a = {k: np.asarray(v) for k, v in inputs.items()}
    att = {k[len("L0_attn_"):]: v for k, v in a.items() if k.startswith("L0_attn_")}
    ffn = [{k[len("L0_ffn_q_"):]: v for k, v in a.items() if k.startswith(f"L0_ffn_{f}_")} for f in "qkv"]

    def chunks(m):
        return m.reshape(-1, P, m.shape[1]).transpose(1, 0, 2)

    wq, wk, wv = (chunks(att[k]) for k in ("Wq", "Wk", "Wv"))
    count, unit = tree_constants()
    b2 = np.zeros((P, NFFF, DIM), np.float32)
    for f in range(NFFF):
        b2[f * LEAVES:(f + 1) * LEAVES, f] = ffn[f]["b2"]
    pick = np.zeros((3 * PARTS, PARTS, SEQ), np.float32)
    for j in range(PARTS):
        pick[3 * j:3 * j + 3, j] = 1.0
    return {
        "x": att["x"],
        "wqk": np.stack([np.stack([wq[:, :, t * P:(t + 1) * P], wk[:, :, t * P:(t + 1) * P]], 2) for t in range(4)]),
        "wv": np.stack([wv[:, :, t * 64:(t + 1) * 64] for t in range(4)]),
        "wo": chunks(att["Wo"]),
        "lq1": att["lambda_q1"], "lk1": att["lambda_k1"], "lq2": att["lambda_q2"], "lk2": att["lambda_k2"],
        "gamma": att["gamma"], "beta": att["beta"],
        "nodeT": chunks(np.concatenate([p["node_w"].T for p in ffn], 1)),
        "nodeb": np.concatenate([p["node_b"] for p in ffn])[:, None],
        "w1": np.stack([chunks(p["w1"].transpose(1, 0, 2).reshape(DIM, HID)) for p in ffn]),
        "w2": np.stack([chunks(p["w2"].reshape(HID, DIM)) for p in ffn], 1),
        "b1": np.concatenate([p["b1"].reshape(HT, P).T for p in ffn], 1),
        "b2": b2,
        "off_leaf": unit.astype(bf16),
        "off_count": count.astype(bf16),
        "pick": pick.astype(bf16),
        "ident": np.eye(P, dtype=np.float32),
        "identb": np.eye(P, dtype=np.float32).astype(bf16),
    }


def kernel(**inputs):
    import concourse.bacc as _bacc
    from concourse.bass_utils import run_bass_kernel_spmd as _run

    nc = _bacc.Bacc("TRN2", target_bir_lowering=False, num_devices=1)
    arrays, args = {}, {}
    for name, value in laid_out(inputs).items():
        value = np.ascontiguousarray(value)
        arrays[f"in_{name}"] = value
        args[name] = nc.dram_tensor(f"in_{name}", value.shape, mybir.dt.from_np(value.dtype),
                                    kind="ExternalInput").ap()
    args["out"] = nc.dram_tensor("out_0", (BATCH, SEQ, DIM), F32, kind="ExternalOutput").ap()
    build(nc, args)
    r = _run(nc, [arrays], core_ids=[0])
    return r.results[0]["out_0"]
```

```python
import math
from contextlib import ExitStack

import numpy as np

import concourse.bass as bass
from concourse import mybir

F32 = mybir.dt.float32
BF16 = mybir.dt.bfloat16
F32R = mybir.dt.float32r
ALU = mybir.AluOpType
ACT = mybir.ActivationFunctionType
AX = mybir.AxisListType

P = 128
BATCH, SEQ, DIM = 8, 1024, 256
KC = DIM // P
TT = SEQ // P
CH = 512
NCH = SEQ // CH

NFFF, LEAVES, NODES, LEAF_W, DEPTH = 3, 16, 15, 64, 4
HID = LEAVES * LEAF_W
HT = HID // P
BIG = 2.0 ** 100

HEADS, HD = 16, 16
PARTS = 4
SETS = BATCH * HEADS // 2
TERM_Q = (0, 0, 0, 1, 1, 2)
TERM_K = (0, 1, 2, 0, 1, 0)
TERMS = len(TERM_Q)
KS = TERMS * HD
KM = KS + 3 * PARTS
RING = 4
STEPS = NCH * TT
SCALE = HD ** -0.5
LN_EPS = 1e-5
LAMBDA_INIT = 0.8 - 0.6 * math.exp(-0.3 * (12 - 1))
FFN_SCALE = 1.0 / math.sqrt(DIM)


FFN_WORDS, ATTENTION_WORDS = 25850, 50000


class Arena:

    def __init__(self, base):
        self.base, self.at = base, 0

    def take(self, *shape, dt=F32):
        n = int(np.prod(shape))
        words = (n * (2 if dt == BF16 else 4) + 3) // 4
        words = (words + 7) // 8 * 8
        view = self.base[:, self.at:self.at + words]
        self.at += words
        if dt == BF16:
            view = view.bitcast(BF16)
        view = view[:, 0:n]
        if len(shape) > 1:
            names = "abcde"[:len(shape)]
            sizes = {k: v for k, v in zip(names, shape)}
            view = view.rearrange(f"p ({' '.join(names)}) -> p {' '.join(names)}", **sizes)
        return view


class Chain:

    def __init__(self, eng, sem, start=0):
        self.eng, self.sem, self.n = eng, sem, start

    def __call__(self, ins):
        ins.then_inc(self.sem, 1)
        self.n = self.n + 1
        self.eng.wait_ge(self.sem, self.n)


def rstd_newton(nc, link, out, var, guess, tmp):
    link(nc.vector.reciprocal(out, guess))
    link(nc.vector.tensor_tensor(tmp, out, out, ALU.mult))
    link(nc.vector.tensor_tensor(tmp, tmp, var, ALU.mult))
    link(nc.vector.tensor_scalar(tmp, tmp, -0.5, 1.5, ALU.mult, ALU.add))
    link(nc.vector.tensor_tensor(out, out, tmp, ALU.mult))


class Split:

    def __init__(self, nc, ctx, name, shape):
        self.hi = ctx.enter_context(nc.sbuf_tensor(name + "_hi", [P] + shape, F32R))
        self.lo = ctx.enter_context(nc.sbuf_tensor(name + "_lo", [P] + shape, F32R))

    def set_hi(self, nc, at, src):
        return nc.vector.tensor_copy(self.hi[at], src)

    def set_lo(self, nc, at, src):
        return nc.vector.tensor_tensor(self.lo[at], src, self.hi[at].bitcast(F32), ALU.subtract)


def split_matmul(nc, out, a, a_at, b, b_at, start, stop):
    nc.tensor.matmul(out, a.hi[a_at], b.hi[b_at], start=start, stop=False)
    nc.tensor.matmul(out, a.hi[a_at], b.lo[b_at], start=False, stop=False)
    return nc.tensor.matmul(out, a.lo[a_at], b.hi[b_at], start=False, stop=stop)




def ffn_stage(nc, ctx, ps, x, w, scratch):
    w1 = Split(nc, ctx, "w1", [NFFF, KC, HID])
    xnTs = Split(nc, ctx, "xnT", [KC, SEQ])
    qk = Split(nc, ctx, "qk", [2, KC, SEQ])
    sel = ctx.enter_context(nc.sbuf_tensor("sel", [P, SEQ], F32R))
    b2 = ctx.enter_context(nc.sbuf_tensor("b2", [P, NFFF, DIM], F32R))
    ar = Arena(ctx.enter_context(nc.sbuf_tensor("ffn_arena", [P, FFN_WORDS], F32)))
    xs = ar.take(TT, DIM)
    xnT = ar.take(KC, SEQ)
    w2 = ar.take(NFFF, HT, DIM)
    b1 = ar.take(NFFF * HT)
    nodeT = ar.take(KC, NFFF * NODES)
    nodeb = ar.take(1)
    off_leaf = ar.take(NFFF, HT, P, dt=BF16)
    off_count = ar.take(P, dt=BF16)
    ident = ar.take(P)
    bits = ar.take(SEQ, dt=BF16)
    hid_flat = ar.take(2, HT * CH)
    hid = hid_flat.rearrange("p u (t c) -> p u t c", t=HT)
    v = ar.take(TT, DIM)
    prob = hid_flat[:, 0, 0:2 * SEQ].rearrange("p (a b) -> p a b", a=2)
    probT = hid_flat[:, 0, 2 * SEQ:4 * SEQ].rearrange("p (a b c) -> p a b c", a=2, b=TT)
    w1_in = hid_flat.rearrange("p u n -> p (u n)")[:, 0:NFFF * KC * HID].rearrange(
        "p (f k n) -> p f k n", f=NFFF, k=KC)
    b2_at = NFFF * KC * HID
    b2_in = hid_flat.rearrange("p u n -> p (u n)")[:, b2_at:b2_at + NFFF * DIM].rearrange("p (f n) -> p f n", f=NFFF)
    ffn_out = ar.take(TT, DIM)
    stats = ar.take(TT, 6)
    mv = ar.take(TT, 2)
    var, guess, rstd, tmp = ar.take(TT), ar.take(TT), ar.take(TT), ar.take(TT)
    rowmax, nbias, rowsum, rinv = ar.take(2, 1), ar.take(2, 1), ar.take(TT, 1), ar.take(2, 1)

    def sem(name):
        return ctx.enter_context(nc.semaphore("f_" + name))

    weights_in, x_in, xnT_out, ffn_stored = sem("weights_in"), sem("x_in"), sem("xnT_out"), sem("ffn_stored")
    var_ready, guess_ready, xn_ready = sem("var_ready"), sem("guess_ready"), sem("xn_ready")
    ring_a_full, ring_a_used = sem("ring_a_full"), sem("ring_a_used")
    ring_v_full, ring_v_used = sem("ring_v_full"), sem("ring_v_used")
    sum_in = sem("sum_in")
    w_in = [sem(f"w{f}_in") for f in range(NFFF)]
    w1_loaded = [sem(f"w1_{f}_loaded") for f in range(NFFF)]
    weights_split, xnT_split = sem("weights_split"), sem("xnT_split")
    nbias_ready, dchain = sem("nbias_ready"), sem("dchain")
    A_PER = 2 + 2 + NFFF * NCH * HT // 2 + 2 * TT
    V_PER = 2 + 2 + NFFF * NCH * (HT // 2 + 2) + 3 * TT
    LINKS = 5 + 1 + 3 * TT
    assert A_PER % 4 == 0 and V_PER % 4 == 0
    units = [(f, c) for f in range(NFFF) for c in range(NCH)]
    a_sel = 2
    a_hid = 4
    a_att = a_hid + len(units) * HT // 2
    v_bits = 2
    v_first = 4

    def v_hid(u):
        return v_first + u * (HT // 2) + max(u - 1, 0) * 2

    def v_out(u):
        return v_first + min(u + 2, len(units)) * (HT // 2) + u * 2

    v_att = v_first + len(units) * (HT // 2 + 2)

    def bank_a(k):
        return ps[:, (k % 4) * CH:(k % 4) * CH + CH]

    def bank_v(k):
        return ps[:, (4 + k % 4) * CH:(4 + k % 4) * CH + CH]

    def v_prob(t):
        return v_att + 2 * t + max(t - 1, 0)

    def v_value(t):
        return v_prob(t + 1) + 2 if t < TT - 1 else v_value(t - 1) + 1

    N_SMALL = 7
    with nc.Block() as block:

        @block.sync
        def _(sp):
            nc.sync.dma_start(xs, x[0].rearrange("(t p) d -> p t d", p=P)).then_inc(x_in, 16)
            for dst, name in ((nodeT, "nodeT"), (nodeb[0:NFFF * NODES], "nodeb"), (off_leaf, "off_leaf"),
                              (off_count, "off_count"), (ident, "ident"), (b1, "b1"), (b2_in, "b2")):
                nc.sync.dma_start(dst, w[name]).then_inc(weights_in, 16)
            for f in range(NFFF):
                nc.sync.dma_start(w1_in[:, f], w["w1"][f]).then_inc(w1_loaded[f], 16)
            for f in range(NFFF):
                nc.sync.dma_start(w2[:, f], w["w2"][f]).then_inc(w_in[f], 16)
            with sp.Fori(0, BATCH) as b:
                sp.wait_ge(ring_a_used, b * A_PER + 2 + 4)
                sp.wait_ge(ring_v_used, b * V_PER + 2 + 4)
                nc.sync.dma_start(xs, x[(b + 1) % BATCH].rearrange("(t p) d -> p t d", p=P)).then_inc(x_in, 16)
                nc.sync.dma_start(scratch["xnT"][b], xnT).then_inc(xnT_out, 16)
                sp.wait_ge(ffn_stored, b * 16 + 1)
                nc.sync.dma_start(ffn_out, x[b].rearrange("(t p) d -> p t d", p=P)).then_inc(sum_in, 16)
                sp.wait_ge(ring_v_used, b * V_PER + V_PER + 4)
                nc.sync.dma_start(scratch["ffn"][b].rearrange("(t p) d -> p t d", p=P), ffn_out).then_inc(ffn_stored, 16)
            sp.wait_ge(x_in, 16 * (BATCH + 1))
            sp.wait_ge(xnT_out, 16 * BATCH + 1)
            sp.wait_ge(ffn_stored, 16 * BATCH + 1)

        @block.tensor
        def _(pe):
            pe.wait_ge(weights_in, 16 * N_SMALL)
            with pe.Fori(0, BATCH) as b:
                def take_a(k):
                    pe.wait_ge(ring_a_used, b * A_PER + k + 1)
                    return bank_a(k)

                def take_v(k):
                    pe.wait_ge(ring_v_used, b * V_PER + k + 1)
                    return bank_v(k)

                pe.wait_ge(xn_ready, b + 1)
                for k in range(KC):
                    for half in range(2):
                        bank = (take_a if half else take_v)(k)
                        for q in range(4):
                            last = nc.tensor.transpose(bank[:, q * P:(q + 1) * P],
                                                       xs[:, half * 4 + q, k * P:(k + 1) * P], ident)
                        last.then_inc(ring_a_full if half else ring_v_full, 1)
                pe.wait_ge(ring_a_used, b * A_PER + 2 + 4)
                pe.wait_ge(ring_v_used, b * V_PER + 2 + 4)
                for c in range(NCH):
                    bank = take_v(v_bits + c)
                    for k in range(KC):
                        last = nc.tensor.matmul(bank[0:NFFF * NODES, :], nodeT[:, k, :],
                                                xnT[:, k, c * CH:(c + 1) * CH], start=k == 0, stop=k == KC - 1)
                    last.then_inc(ring_v_full, 1)
                for c in range(NCH):
                    pe.wait_ge(ring_v_used, b * V_PER + v_bits + c + 1 + 4)
                    nc.tensor.matmul(take_a(a_sel + c), off_count, bits[:, c * CH:(c + 1) * CH],
                                     start=True, stop=True).then_inc(ring_a_full, 1)

                def hidden(u):
                    f, c = units[u]
                    pe.wait_ge(xnT_split, b * NCH + (c + 1))
                    pe.wait_ge(weights_split, NFFF + 1)
                    for t in range(HT):
                        odd = t % 2
                        k = t // 2 + (v_hid(u) if odd else a_hid + u * (HT // 2))
                        bank = (take_v if odd else take_a)(k)
                        cols = slice(c * CH, (c + 1) * CH)
                        nc.tensor.matmul(bank, off_leaf[:, f, t, :], bits[:, cols], start=True, stop=False)
                        for kc in range(KC):
                            last = split_matmul(nc, bank, w1, np.s_[:, f, kc, t * P:(t + 1) * P],
                                                xnTs, np.s_[:, kc, cols], False, kc == KC - 1)
                        last.then_inc(ring_v_full if odd else ring_a_full, 1)

                def out(u):
                    f, c = units[u]
                    pe.wait_ge(w_in[f], 16)
                    pe.wait_ge(ring_a_used, b * A_PER + a_hid + (u + 1) * (HT // 2) + 4)
                    pe.wait_ge(ring_v_used, b * V_PER + v_hid(u) + HT // 2 + 4)
                    for m in range(2):
                        bank = take_v(v_out(u) + m)
                        if f < 2:
                            for t in range(HT):
                                nc.tensor.matmul(bank, w2[:, f, t, m * P:(m + 1) * P], hid[:, u % 2, t, :],
                                                 start=t == 0, stop=False)
                            last = nc.tensor.matmul(bank, b2[:, f, m * P:(m + 1) * P], sel[:, c * CH:(c + 1) * CH],
                                                    start=False, stop=True)
                        else:
                            for j in range(2):
                                tok = (2 * m + j) * P
                                o = bank[:, j * DIM:(j + 1) * DIM]
                                for t in range(HT):
                                    nc.tensor.matmul(o, hid[:, u % 2, t, tok:tok + P], w2[:, f, t, :],
                                                     start=t == 0, stop=False)
                                last = nc.tensor.matmul(o, sel[:, c * CH + tok:c * CH + tok + P], b2[:, f, :],
                                                        start=False, stop=True)
                        last.then_inc(ring_v_full, 1)

                hidden(0)
                for u in range(len(units)):
                    if u + 1 < len(units):
                        hidden(u + 1)
                    out(u)

                pe.wait_ge(ring_v_used, b * V_PER + v_att + 4)

                def scores(t):
                    for c in range(NCH):
                        bank = take_a(a_att + 2 * t + c)
                        for k in range(KC):
                            last = split_matmul(nc, bank, qk, np.s_[:, 0, k, t * P:(t + 1) * P],
                                                qk, np.s_[:, 1, k, c * CH:(c + 1) * CH], k == 0, k == KC - 1)
                        last.then_inc(ring_a_full, 1)

                def turn(t):
                    pe.wait_ge(ring_a_used, b * A_PER + a_att + 2 * t + 2 + 4)
                    for h in range(2):
                        bank = take_v(v_prob(t) + h)
                        for q in range(4):
                            kt = 4 * h + q
                            last = nc.tensor.transpose(bank[:, q * P:(q + 1) * P],
                                                       prob[:, t % 2, kt * P:(kt + 1) * P], ident)
                        last.then_inc(ring_v_full, 1)

                def values(t):
                    pe.wait_ge(ring_v_used, b * V_PER + v_prob(t) + 2 + 4)
                    bank = take_v(v_value(t))
                    for kt in range(TT):
                        last = nc.tensor.matmul(bank[:, 0:DIM], probT[:, t % 2, kt, :], v[:, kt, :],
                                                start=kt == 0, stop=kt == TT - 1)
                    last.then_inc(ring_v_full, 1)

                scores(0)
                for t in range(TT):
                    if t + 1 < TT:
                        scores(t + 1)
                    turn(t)
                    if t > 0:
                        values(t - 1)
                values(TT - 1)

        @block.scalar
        def _(act):
            act.wait_ge(var_ready, 1)
            nc.scalar.activation(guess, var, ACT.Sqrt).then_inc(guess_ready, 1)
            act.wait_ge(weights_in, 16 * N_SMALL)
            act.wait_ge(weights_split, NFFF + 1)
            with act.Fori(0, BATCH) as b:
                def full(k):
                    act.wait_ge(ring_a_full, b * A_PER + k + 1)
                    return bank_a(k)

                act.wait_ge(xnT_out, b * 16 + 1)
                for k in range(KC):
                    nc.scalar.activation(xnT[:, k, CH:SEQ], full(k), ACT.Copy).then_inc(ring_a_used, 1)
                for c in range(NCH):
                    nc.scalar.activation(sel[:, c * CH:(c + 1) * CH], full(a_sel + c), ACT.Relu,
                                         scale=-1.0, bias=1.0).then_inc(ring_a_used, 1)
                for u, (f, c) in enumerate(units):
                    for t in range(0, HT, 2):
                        nc.scalar.activation(hid[:, u % 2, t, :], full(a_hid + u * (HT // 2) + t // 2), ACT.Relu,
                                             bias=b1[:, f * HT + t:f * HT + t + 1]).then_inc(ring_a_used, 1)
                act.wait_ge(var_ready, b + 2)
                nc.scalar.activation(guess, var, ACT.Sqrt).then_inc(guess_ready, 1)
                for t in range(TT):
                    full(a_att + 2 * t + 1)
                    act.wait_ge(nbias_ready, b * TT + t + 1)
                    if t >= 2:
                        act.wait_ge(ring_v_used, b * V_PER + v_prob(t - 2) + 2 + 4)
                    bk = (a_att + 2 * t) % 4 * CH
                    nc.scalar.activation(prob[:, t % 2, :], ps[:, bk:bk + SEQ], ACT.Exp, scale=FFN_SCALE,
                                         bias=nbias[:, t % 2], accum_out=rowsum[:, t]).then_inc(ring_a_used, 2)

        @block.vector
        def _(dve):
            link0 = Chain(dve, dchain)

            def norm_stats(link, bb):
                dve.wait_ge(x_in, bb * 16 + 16)
                for t in range(TT):
                    ins = nc.vector.bn_stats(stats[:, t, :], xs[:, t, :])
                link(ins)
                nc.vector.memset(tmp, 0.0)
                for t in range(TT):
                    ins = nc.vector.bn_aggr(mv[:, t, :], stats[:, t, :])
                link(ins)
                nc.vector.tensor_scalar(var, mv[:, :, 1], LN_EPS, None, ALU.add).then_inc(var_ready, 1)

            def norm_apply(link, bb):
                dve.wait_ge(guess_ready, bb + 1)
                rstd_newton(nc, link, rstd, var, guess, tmp)
                for t in range(TT):
                    ins = nc.vector.tensor_scalar(xs[:, t, :], xs[:, t, :], mv[:, t, 0:1], rstd[:, t:t + 1],
                                                  ALU.subtract, ALU.mult)
                ins.then_inc(xn_ready, 1)

            link0(nc.vector.memset(bits, 1.0))
            nc.vector.memset(rowsum, 0.0).then_inc(ring_a_used, 4)
            nc.vector.memset(rowmax, 0.0).then_inc(ring_v_used, 4)
            nc.vector.memset(nbias, 0.0).then_inc(xnT_out, 1)
            nc.vector.memset(rinv, 0.0).then_inc(ffn_stored, 1)
            norm_stats(link0, 0)
            norm_apply(link0, 0)
            dve.wait_ge(weights_in, 16 * N_SMALL)
            link0(nc.vector.tensor_copy(b2[:], b2_in))
            nc.vector.tensor_tensor(b2[P // 2:P], b2_in[P // 2:P], b2[P // 2:P].bitcast(F32), ALU.subtract
                                    ).then_inc(weights_split, 1)
            for f in range(NFFF):
                dve.wait_ge(w1_loaded[f], 16)
                link0(w1.set_hi(nc, np.s_[:, f], w1_in[:, f]))
                w1.set_lo(nc, np.s_[:, f], w1_in[:, f]).then_inc(weights_split, 1)
            dve.wait_ge(weights_split, NFFF + 1)
            n0 = link0.n
            per_batch = 2 + 5 + TT * 2 + NCH + 2 * 2 * NCH

            with dve.Fori(0, BATCH) as b:
                link = Chain(dve, dchain, b * per_batch + n0)

                def full(k):
                    dve.wait_ge(ring_v_full, b * V_PER + k + 1)
                    return bank_v(k)

                dve.wait_ge(xnT_out, b * 16 + 1)
                for k in range(KC):
                    nc.vector.tensor_copy(xnT[:, k, 0:CH], full(k)).then_inc(ring_v_used, 1)
                for c in range(NCH):
                    nc.vector.tensor_scalar(bits[0:NFFF * NODES, c * CH:(c + 1) * CH],
                                            full(v_bits + c)[0:NFFF * NODES, :], nodeb[0:NFFF * NODES], 0.0,
                                            ALU.add, ALU.is_ge).then_inc(ring_v_used, 1)

                dve.wait_ge(ring_a_used, b * A_PER + 2 + 4)
                for c in range(NCH):
                    cols = np.s_[:, :, c * CH:(c + 1) * CH]
                    link(xnTs.set_hi(nc, cols, xnT[cols]))
                    xnTs.set_lo(nc, cols, xnT[cols]).then_inc(xnT_split, 1)

                def hidden(u):
                    f, c = units[u]
                    for t in range(1, HT, 2):
                        nc.vector.tensor_scalar(hid[:, u % 2, t, :], full(v_hid(u) + t // 2),
                                                b1[:, f * HT + t:f * HT + t + 1], 0.0, ALU.add, ALU.max
                                                ).then_inc(ring_v_used, 1)

                def out(u):
                    f, c = units[u]
                    for m in range(2):
                        src = full(v_out(u) + m)
                        if f < 2:
                            dst = np.s_[:, f, m, c * CH:(c + 1) * CH]
                            link(qk.set_hi(nc, dst, src))
                            qk.set_lo(nc, dst, src).then_inc(ring_v_used, 1)
                        else:
                            dst = v[:, 4 * c + 2 * m:4 * c + 2 * m + 2, :].rearrange("p t d -> p (t d)")
                            nc.vector.tensor_copy(dst, src).then_inc(ring_v_used, 1)

                hidden(0)
                for u in range(len(units)):
                    if u + 1 < len(units):
                        hidden(u + 1)
                    out(u)
                    if u == 2:
                        norm_stats(link, b + 1)

                def row_max(t):
                    dve.wait_ge(ring_a_full, b * A_PER + a_att + 2 * t + 2)
                    bk = (a_att + 2 * t) % 4 * CH
                    link(nc.vector.tensor_reduce(rowmax[:, t % 2], ps[:, bk:bk + SEQ], AX.X, ALU.max))
                    nc.vector.tensor_scalar(nbias[:, t % 2], rowmax[:, t % 2], -FFN_SCALE, None, ALU.mult
                                            ).then_inc(nbias_ready, 1)

                def value(t):
                    link(nc.vector.reciprocal(rinv[:, t % 2], rowsum[:, t]))
                    nc.vector.scalar_tensor_tensor(ffn_out[:, t, :], full(v_value(t))[:, 0:DIM], rinv[:, t % 2],
                                                   ffn_out[:, t, :], ALU.mult, ALU.add).then_inc(ring_v_used, 1)

                row_max(0)
                dve.wait_ge(sum_in, b * 16 + 16)
                for t in range(TT):
                    if t + 1 < TT:
                        row_max(t + 1)
                    for h in range(2):
                        nc.vector.tensor_copy(probT[:, t % 2, 4 * h:4 * h + 4, :].rearrange("p a b -> p (a b)"),
                                              full(v_prob(t) + h)).then_inc(ring_v_used, 1)
                    if t > 0:
                        value(t - 1)
                    if t == 3:
                        norm_apply(link, b + 1)
                value(TT - 1)




def attention_stage(nc, ctx, base, ps, w, scratch, out):
    ar = Arena(base)
    ring = ar.take(RING, 2, PARTS, SEQ, dt=BF16)
    split = ar.take(2, 3, SEQ, dt=BF16)
    rest = ar.take(2, SEQ)
    xnT = ar.take(KC, SEQ)
    wqk = ar.take(KC, 2, P)
    wv = ar.take(KC, PARTS * HD)
    vaug = ar.take(2, TT, 4, 32)
    prob = ar.take(2, PARTS, CH)
    osb = ar.take(NCH, CH)
    ident = ar.take(P)
    identb = ar.take(P, dt=BF16)
    omul = ar.take(4, PARTS, HD)
    linv = ar.take(4, PARTS)
    oset = ar.take(TT, P)
    halfmax = ar.take(PARTS, TT, NCH)
    smax = ar.take(PARTS, TT)
    mrest = ar.take(PARTS, TT)
    mparts = ar.take(TT, PARTS, 3, dt=BF16)
    mrow = ar.take(SEQ, dt=BF16)
    zeros = ar.take(SEQ, dt=BF16)
    lam_in = ar.take(4, HD)
    lam_prod = ar.take(HD)
    lam_dot, lam_exp, lam = ar.take(2), ar.take(2), ar.take(1)
    sign = ar.take(4, PARTS)
    proj = OutputGroup(nc, ctx, ar, "a_")

    def sem(name):
        return ctx.enter_context(nc.semaphore("a_" + name))

    o_zeroed, o_zero_stored, group_in, group_out = (
        sem("o_zeroed"), sem("o_zero_stored"), sem("group_in"), sem("group_out"))

    consts_in, lam_loaded = sem("consts_in"), sem("lam_loaded")
    tile_in = sem("tile_in")
    split_stored = sem("split_stored")
    slot_in = [sem(f"slot{s}_in") for s in range(RING)]
    oset_stored = sem("oset_stored")
    lam_dots, lam_exps = sem("lam_dots"), sem("lam_exps")
    aux_full, aux_used = sem("aux_full"), sem("aux_used")
    score_full, exp_done = sem("score_full"), sem("exp_done")
    value_done, value_copied, oturned = sem("value_done"), sem("value_copied"), sem("oturned")
    split_ready, oset_ready = sem("split_ready"), sem("oset_ready")
    mparts_ready, shift_ready = sem("mparts_ready"), sem("shift_ready")
    zeros_ready = sem("zeros_ready")
    dchain, pchain = sem("dchain"), sem("pchain")

    score = ps[:, 0:4 * CH].rearrange("p (a b) -> p a b", a=PARTS)
    value_bank = ps[:, 4 * CH:5 * CH]
    AUX = 3
    aux_bank = [ps[:, (5 + n) * CH:(6 + n) * CH] for n in range(AUX)]
    aux_bf16 = [a.bitcast(BF16) for a in aux_bank]
    ITERS = SETS // RING
    SCORES = 2 * STEPS * RING

    V_TILES = ((0, TT),)

    def extras(s, step, tail):
        out = []
        if step == 1 and s % 2 == 0 and not (tail and s == 2):
            out += [("v", n) for n in range(len(V_TILES))]
        if step in (1, 2, 3, 4) and s % 2 == 1 and not tail:
            out.append(("qk", step - 1))
        if step == 2 and not (tail and s == 3):
            out.append(("shift", 0))
        if step == 4 and s > 0:
            out.append(("o", 1))
        if step == 11:
            out.append(("o", 0))
        if s == 2 and step in (5, 6, 8, 9):
            out.append(("turn" if step < 8 else "out", step % 5 if step < 8 else step - 8))
        if not (tail and s >= 2):
            out += [("max", 4 * step + n) for n in range(4)]
        if s == RING - 1 and step == STEPS - 1:
            out.append(("o", 2))
        return out

    def uses_before(s, step, kind, number, tail=False):
        count = 0
        for s2 in range(RING):
            for step2 in range(STEPS):
                for one in extras(s2, step2, tail):
                    count += 1
                    if (s2, step2, one) == (s, step, (kind, number)):
                        return count
        return count

    MAXIMA = PARTS * TT * NCH
    PROLOGUE = [("qk", 0, n) for n in range(4)] + [("v", 0, n) for n in range(len(V_TILES))] + [("qk", 1, n) for n in range(4)] + \
        [("max", 0, n) for n in range(MAXIMA)] + [("shift", 0, 0)] + [("max", 1, n) for n in range(MAXIMA)]
    PRO = len(PROLOGUE)
    PER_ITER = uses_before(RING, 0, "", 0)
    LAST_V = len(V_TILES) - 1
    assert PER_ITER % AUX == 0

    with nc.Block() as block:

        @block.sync
        def _(sp):
            def load_tile(t, odd):
                if not odd:
                    nc.sync.dma_start(xnT, scratch["xnT"][t // 4]).then_inc(tile_in, 16)
                nc.sync.dma_start(wqk, w["wqk"][t % 4]).then_inc(tile_in, 16)
                nc.sync.dma_start(wv, w["wv"][t % 4]).then_inc(tile_in, 16)

            def store_split(t):
                sp.wait_ge(split_ready, t * 4 + 4)
                for a in range(2):
                    nc.sync.dma_start(scratch["split"][t, a].rearrange("s p t -> p s t"), split[:, a]
                                      ).then_inc(split_stored, 16)
                sp.wait_ge(split_stored, t * 32 + 32)

            def load_set(t, half, slot):
                for a, parts in enumerate((TERM_Q, TERM_K)):
                    for i, part in enumerate(parts):
                        src = scratch["split"][t, a, part, 64 * half:64 * half + 64, :]
                        nc.sync.dma_start(ring[HD * i:HD * (i + 1), slot, a],
                                          src.rearrange("(j d) t -> d j t", d=HD)).then_inc(slot_in[slot], 16)

            load_tile(0, False)
            for n, name in enumerate(("lq1", "lk1", "lq2", "lk2")):
                nc.sync.dma_start(lam_in[:, n], w[name].partition_broadcast(P)).then_inc(lam_loaded, 16)
            nc.sync.dma_start(ident, w["ident"]).then_inc(consts_in, 16)
            nc.sync.dma_start(identb, w["identb"]).then_inc(consts_in, 16)
            for s in range(RING):
                nc.sync.dma_start(ring[KS:KM, s, 1], w["pick"]).then_inc(consts_in, 16)
            proj.load_consts(nc.sync, w, consts_in)
            store_split(0)
            load_set(0, 0, 0)
            load_set(0, 1, 1)
            sp.wait_ge(aux_used, PROLOGUE.index(("v", 0, LAST_V)) + 1 + AUX)
            load_tile(1, True)
            store_split(1)
            load_set(1, 0, 2)

            sp.wait_ge(o_zeroed, 1)
            for n in range(4):
                nc.sync.dma_start(scratch["o"][n].rearrange("t p d -> p t d"), oset[:, 0:4]
                                  ).then_inc(o_zero_stored, 16)
            sp.wait_ge(o_zero_stored, 64)

            def body(i, tail):
                group = (i + (2 * BATCH - 2)) % (2 * BATCH)
                o_at = i // 2 * 4 + i % 2 + 4
                if not tail:
                    group, o_at = sp.snap(group), sp.snap(o_at)
                for s in range(RING):
                    sp.wait_ge(score_full, i * SCORES + (2 * STEPS * s + 1))
                    if s % 2 == 0:
                        if not (tail and s == 2):
                            load_set(i * 2 + (s // 2 + 1), 1, (s + 3) % RING)
                        if not tail:
                            sp.wait_ge(aux_used, i * PER_ITER + (PRO + AUX + uses_before(s, 1, "v", LAST_V)))
                            load_tile(i * 2 + (s // 2 + 2), s == 2)
                    elif not tail:
                        store_split(i * 2 + (s // 2 + 2))
                        load_set(i * 2 + (s // 2 + 2), 0, (s + 3) % RING)
                    if s == 1:
                        sp.wait_ge(oset_stored, i * 32 + 1)
                        proj.load(nc.sync, scratch, i, group, group_in)
                sp.wait_ge(proj.y_ready, i + 2)
                proj.store(nc.sync, out, group, group_out)
                sp.wait_ge(oset_ready, i * (2 * RING) + (2 * RING + 2))
                for h in range(2):
                    nc.sync.dma_start(scratch["o"][o_at + 2 * h].rearrange("t p d -> p t d"), oset[:, 4 * h:4 * h + 4]
                                      ).then_inc(oset_stored, 16)

            with sp.Fori(0, ITERS - 1) as i:
                body(i, False)
            body(ITERS - 1, True)
            sp.wait_ge(oset_stored, 32 * ITERS + 1)
            sp.wait_ge(group_out, 16 * ITERS + 1)

        @block.tensor
        def _(pe):
            def aux(k):
                pe.wait_ge(aux_used, k + 1)

            def project_qk(i, n, number, bank):
                a, c = number // 2, number % 2
                pe.wait_ge(tile_in, i * 80 + (n // 2 * 80 + (80 if n % 2 else 48)))
                for kc in range(KC):
                    last = nc.tensor.matmul(aux_bank[bank], wqk[:, kc, a, :], xnT[:, kc, c * CH:(c + 1) * CH],
                                            start=kc == 0, stop=kc == KC - 1)
                last.then_inc(aux_full, 1)

            def project_v(number, bank):
                first, end = V_TILES[number]
                for tt in range(first, end):
                    for kc in range(KC):
                        last = nc.tensor.matmul(aux_bank[bank][:, (tt - first) * 64:(tt - first + 1) * 64],
                                                xnT[:, kc, tt * P:(tt + 1) * P], wv[:, kc, :],
                                                start=kc == 0, stop=kc == KC - 1)
                last.then_inc(aux_full, 1)

            def row_scores(number, slot, bank):
                j, qt, c = number // (TT * NCH), number // NCH % TT, number % NCH
                nc.tensor.matmul(aux_bank[bank], ring[0:KS, slot, 0, j, qt * P:(qt + 1) * P],
                                 ring[0:KS, slot, 1, j, c * CH:(c + 1) * CH], start=True, stop=True
                                 ).then_inc(aux_full, 1)

            def turn_shift(n, bank):
                pe.wait_ge(mparts_ready, n + 1)
                for qt in range(TT):
                    last = nc.tensor.transpose(aux_bf16[bank][KS:KM, qt * P:(qt + 1) * P],
                                               mparts[:, qt].rearrange("p a b -> p (a b)"), identb,
                                               tile_position=(0, KS))
                last.then_inc(aux_full, 1)

            def turn_o(c, n, bank):
                pe.wait_ge(value_copied, n * 2 + (c + 1 + 2))
                for q in range(4):
                    last = nc.tensor.transpose(aux_bank[bank][:, q * P:(q + 1) * P], osb[:, c, q * P:(q + 1) * P],
                                               ident)
                last.then_inc(aux_full, 1)

            def scores(i, s, step, h):
                c, kt = step // TT, step % TT
                g = 2 * (STEPS * s + step)
                if step == 0 and h == 0:
                    pe.wait_ge(shift_ready, i * RING + (s + 1))
                pe.wait_ge(exp_done, i * SCORES + (g + h + 1))
                for j in (2 * h, 2 * h + 1):
                    last = nc.tensor.matmul(score[:, j, :], ring[0:KM, s, 1, j, kt * P:(kt + 1) * P],
                                            ring[0:KM, s, 0, j, c * CH:(c + 1) * CH], start=True, stop=True)
                last.then_inc(score_full, 1)

            def values(i, s, step):
                c, kt = step // TT, step % TT
                pe.wait_ge(exp_done, i * SCORES + (2 * (STEPS * s + step) + 2 + 2))
                if kt == 0:
                    pe.wait_ge(value_copied, i * (2 * RING) + (2 * s + c + 2))
                for j in range(PARTS):
                    last = nc.tensor.matmul(value_bank[32 * j:32 * j + 32, :],
                                            vaug[:, s // 2, kt, 2 * (s % 2) + j // 2, :], prob[:, step % 2, j, :],
                                            start=kt == 0, stop=kt == TT - 1, tile_position=(0, 32 * j))
                last.then_inc(value_done, 1)

            for k, (kind, n, number) in enumerate(PROLOGUE):
                aux(k)
                if kind == "qk":
                    project_qk(0, n, number, k % AUX)
                elif kind == "v":
                    project_v(number, k % AUX)
                elif kind == "shift":
                    turn_shift(n, k % AUX)
                else:
                    if number == 0:
                        if n == 0:
                            pe.wait_ge(consts_in, 16 * (2 + RING + 3))
                        pe.wait_ge(slot_in[n], 12 * 16)
                    row_scores(number, n, k % AUX)

            def body(i, tail):
                k = 0
                for s in range(RING):
                    for step in range(STEPS):
                        todo = extras(s, step, tail)
                        scores_at, values_at = len(todo) // 4, len(todo) // 2
                        scores(i, s, step, 0)
                        for n, (kind, number) in enumerate(todo + [("", 0)]):
                            if n == scores_at:
                                scores(i, s, step, 1)
                            if n == values_at:
                                if step > 0:
                                    values(i, s, step - 1)
                                elif s > 0:
                                    values(i, s - 1, STEPS - 1)
                            if kind == "":
                                break
                            if (kind, number) == ("o", 2):
                                values(i, s, step)
                            aux(i * PER_ITER + (PRO + k))
                            bank = (PRO + k) % AUX
                            k += 1
                            if kind == "v":
                                project_v(number, bank)
                            elif kind == "qk":
                                project_qk(i, s // 2 + 2, number, bank)
                            elif kind == "shift":
                                turn_shift(i * RING + (s + 1), bank)
                            elif kind == "turn":
                                if number == 0:
                                    pe.wait_ge(group_in, i * 48 + 48)
                                proj.turn(nc, aux_bank[bank], number, ident).then_inc(aux_full, 1)
                            elif kind == "out":
                                turned = uses_before(s, 5 + number, "turn", number, tail)
                                pe.wait_ge(aux_used, i * PER_ITER + (PRO + AUX + turned))
                                proj.project(nc, aux_bank[bank], number).then_inc(aux_full, 1)
                            elif kind == "o":
                                turn_o(0 if number == 0 else 1, i * RING + (s - 1 if number == 1 else s), bank)
                            else:
                                if number == 0:
                                    pe.wait_ge(slot_in[(s + 2) % RING], i * 192 + 192 * (1 + (s + 2) // RING))
                                row_scores(number, (s + 2) % RING, bank)

            with pe.Fori(0, ITERS - 1) as i:
                body(i, False)
            body(ITERS - 1, True)

        @block.scalar
        def _(act):
            act.wait_ge(lam_dots, 1)
            nc.scalar.activation(lam_exp, lam_dot, ACT.Exp).then_inc(lam_exps, 1)

            def copy_values(i, s, c):
                act.wait_ge(value_done, i * (STEPS * RING) + (STEPS * s + TT * (c + 1) + 2))
                act.wait_ge(oset_ready, i * (2 * RING) + (2 * s + c + 1))
                nc.scalar.activation(osb[:, c, :], value_bank, ACT.Copy).then_inc(value_copied, 1)

            def body(i):
                for s in range(RING):
                    for step in range(STEPS):
                        g = STEPS * s + step
                        act.wait_ge(value_done, i * (STEPS * RING) + (g + 1))
                        for h in range(2):
                            act.wait_ge(score_full, i * SCORES + (2 * g + h + 2))
                            nc.scalar.activation(prob[:, step % 2, 2 * h:2 * h + 2, :], score[:, 2 * h:2 * h + 2, :],
                                                 ACT.Exp, scale=SCALE).then_inc(exp_done, 1)
                        if step == TT:
                            copy_values(i, s, 0)
                        if step == 0 and s > 0:
                            copy_values(i, s - 1, 1)
                        if s == 2 and step == STEPS - 3:
                            act.wait_ge(proj.var_ready, i + 1)
                            proj.guess_std(nc)
                copy_values(i, RING - 1, 1)

            with act.Fori(0, ITERS) as i:
                body(i)

        @block.gpsimd
        def _(pool):
            def split_rest(t, used):
                for number in range(4):
                    a, c = number // 2, number % 2
                    cols = slice(c * CH, (c + 1) * CH)
                    pool.wait_ge(aux_used, used(number))
                    nc.gpsimd.tensor_tensor(split[:, a, 1, cols], rest[:, a, cols], zeros[:, 0:CH], ALU.add
                                            ).then_inc(pchain, 1)
                    pool.wait_ge(pchain, t * 4 + (number + 1))
                    nc.gpsimd.tensor_tensor(split[:, a, 2, cols], rest[:, a, cols], split[:, a, 1, cols],
                                            ALU.subtract).then_inc(split_ready, 1)

            def place_shift(slot, used, splits, groups=None):
                pool.wait_ge(split_ready, splits)
                if groups is not None:
                    pool.wait_ge(proj.y_ready, groups + 1)
                pool.wait_ge(aux_used, used)
                for j in range(PARTS):
                    last = nc.gpsimd.tensor_tensor(ring[KS:KM, slot, 0, j, :], mrow[KS:KM, :], zeros[KS:KM, :], ALU.add)
                last.then_inc(shift_ready, 1)

            pool.wait_ge(zeros_ready, 1)
            for t in range(2):
                split_rest(t, lambda number: PROLOGUE.index(("qk", t, number)) + 1 + AUX)
            place_shift(0, PROLOGUE.index(("shift", 0, 0)) + 1 + AUX, 8)

            def body(i, tail):
                def used(s, step, kind, number):
                    return i * PER_ITER + (PRO + AUX + uses_before(s, step, kind, number, tail))

                for s in range(RING):
                    if not (tail and s == RING - 1):
                        place_shift((s + 1) % RING, used(s, 2, "shift", 0),
                                    ITERS * 8 if tail else i * 8 + (8 + s // 2 * 4), i)
                    if s % 2 == 1 and not tail:
                        pool.wait_ge(shift_ready, i * RING + (s + 2))
                        split_rest(i * 2 + (s // 2 + 2), lambda number: used(s, 1 + number, "qk", number))
                pool.wait_ge(group_in, i * 48 + 48)
                proj.finish_pool(nc, pool, i)

            with pool.Fori(0, ITERS - 1) as i:
                body(i, False)
            body(ITERS - 1, True)

        @block.vector
        def _(dve):
            link = Chain(dve, dchain)
            nc.vector.memset(lam[:, 0:1], 0.0).then_inc(aux_used, AUX)
            nc.vector.memset(sign[:, :, 0], 1.0).then_inc(exp_done, 2)
            nc.vector.memset(sign[:, :, 2], 1.0).then_inc(value_done, 2)
            nc.vector.memset(linv, 0.0).then_inc(value_copied, 2)
            nc.vector.memset(omul, 0.0).then_inc(oset_ready, 2)
            nc.vector.memset(halfmax, 0.0).then_inc(score_full, 1)
            nc.vector.memset(smax, 0.0).then_inc(oset_stored, 1)
            nc.vector.memset(mrest, 0.0).then_inc(group_out, 1)
            nc.vector.memset(lam_exp, 0.0).then_inc(proj.y_ready, 1)
            nc.vector.memset(zeros, 0.0).then_inc(zeros_ready, 1)
            nc.vector.memset(oset, 0.0).then_inc(o_zeroed, 1)
            link(nc.vector.memset(vaug, 0.0))
            nc.vector.memset(vaug[:, 0, :, :, HD:HD + 1], 1.0)
            link(nc.vector.memset(vaug[:, 1, :, :, HD:HD + 1], 1.0))
            dve.wait_ge(lam_loaded, 64)
            for n in range(2):
                link(nc.vector.tensor_tensor(lam_prod, lam_in[:, 2 * n], lam_in[:, 2 * n + 1], ALU.mult))
                ins = nc.vector.tensor_reduce(lam_dot[:, n:n + 1], lam_prod, AX.X, ALU.add)
                if n == 0:
                    link(ins)
            ins.then_inc(lam_dots, 1)
            dve.wait_ge(lam_exps, 1)
            link(nc.vector.tensor_tensor(lam, lam_exp[:, 0:1], lam_exp[:, 1:2], ALU.subtract))
            link(nc.vector.tensor_scalar(lam, lam, LAMBDA_INIT, -1.0, ALU.add, ALU.mult))
            for j in (1, 3):
                link(nc.vector.tensor_scalar(sign[:, :, j], linv[:, :, 0], lam, None, ALU.add))

            def full(k):
                dve.wait_ge(aux_full, k + 1)

            def read_qk(link, t, number, bank):
                a, c = number // 2, number % 2
                cols = slice(c * CH, (c + 1) * CH)
                if number == 0 and not (isinstance(t, int) and t == 0):
                    dve.wait_ge(split_stored, t * 32)
                link(nc.vector.tensor_copy(split[:, a, 0, cols], aux_bank[bank]))
                nc.vector.tensor_tensor(rest[:, a, cols], aux_bank[bank], split[:, a, 0, cols], ALU.subtract
                                        ).then_inc(aux_used, 1)

            def read_v(number, slot, bank):
                first, end = V_TILES[number]
                src = aux_bank[bank][:, 0:(end - first) * 64].rearrange("p (t h d) -> p t h d", t=end - first, h=4)
                nc.vector.tensor_copy(vaug[:, slot, first:end, :, 0:HD], src).then_inc(aux_used, 1)

            def read_max(link, number, bank):
                j, qt, c = number // (TT * NCH), number // NCH % TT, number % NCH
                nc.vector.tensor_reduce(halfmax[:, j, qt, c:c + 1], aux_bank[bank], AX.X, ALU.max
                                        ).then_inc(aux_used, 1)

            def split_max(link, uses):
                dve.wait_ge(aux_used, uses)
                link(nc.vector.tensor_reduce(smax, halfmax, AX.X, ALU.max))
                neg = mparts.rearrange("p t j s -> p s j t")
                link(nc.vector.tensor_scalar(neg[:, 0], smax, -1.0, None, ALU.mult))
                link(nc.vector.scalar_tensor_tensor(mrest, smax, -1.0, neg[:, 0], ALU.mult, ALU.subtract))
                link(nc.vector.tensor_copy(neg[:, 1], mrest))
                nc.vector.tensor_tensor(neg[:, 2], mrest, neg[:, 1], ALU.subtract).then_inc(mparts_ready, 1)

            def read_shift(n, bank):
                if not (isinstance(n, int) and n == 0):
                    dve.wait_ge(shift_ready, n)
                nc.vector.tensor_copy(mrow[KS:KM, :], aux_bf16[bank][KS:KM, :]).then_inc(aux_used, 1)

            def read_o(link, i, s, c, k, bank):
                src = aux_bank[bank].rearrange("p (q j d) -> p q j d", q=4, j=PARTS)
                link(nc.vector.reciprocal(linv, src[:, :, :, HD]))
                link(nc.vector.tensor_tensor(linv, linv, sign, ALU.mult))
                nc.vector.tensor_tensor(omul, src[:, :, :, 0:HD], linv.unsqueeze(3).to_broadcast([P, 4, PARTS, HD]),
                                        ALU.mult).then_inc(aux_used, 1)
                dve.wait_ge(aux_used, k + 1 + AUX)
                if s == 0 and c == 0:
                    dve.wait_ge(oset_stored, i * 32 + 1)
                maps = omul.rearrange("p q (h m) d -> p q h m d", m=2)
                dst = oset[:, 4 * c:4 * c + 4, 32 * s:32 * s + 32].rearrange("p q (h d) -> p q h d", h=2)
                nc.vector.tensor_tensor(dst, maps[:, :, :, 0], maps[:, :, :, 1], ALU.add).then_inc(oset_ready, 1)

            for k, (kind, n, number) in enumerate(PROLOGUE):
                full(k)
                if kind == "qk":
                    read_qk(link, n, number, k % AUX)
                elif kind == "v":
                    read_v(number, n, k % AUX)
                elif kind == "shift":
                    read_shift(n, k % AUX)
                else:
                    read_max(link, number, k % AUX)
                    if number == MAXIMA - 1:
                        split_max(link, k + 1 + AUX)
            dve.wait_ge(o_zero_stored, 64)
            links_before = link.n

            def links_in(tail):
                kinds = [e for s in range(RING) for step in range(STEPS) for e in extras(s, step, tail)]
                return sum({"qk": 1, "o": 2}.get(kind, 0) for kind, _ in kinds) + OutputGroup.LINKS + \
                    4 * sum(e == ("max", MAXIMA - 1) for e in kinds)

            per_iter = links_in(False)

            def body(i, tail):
                link = Chain(dve, dchain, i * per_iter + links_before)
                k = 0
                for s in range(RING):
                    for step in range(STEPS):
                        for kind, number in extras(s, step, tail):
                            at = i * PER_ITER + (PRO + k)
                            full(at)
                            bank = (PRO + k) % AUX
                            k += 1
                            if kind == "v":
                                read_v(number, (s // 2 + 1) % 2, bank)
                            elif kind == "qk":
                                read_qk(link, i * 2 + (s // 2 + 2), number, bank)
                            elif kind == "shift":
                                read_shift(i * RING + (s + 1), bank)
                            elif kind == "turn":
                                proj.read_turned(nc, aux_bank[bank], number).then_inc(aux_used, 1)
                            elif kind == "out":
                                if number == 0:
                                    dve.wait_ge(group_out, i * 16 + 1)
                                proj.read_projected(nc, aux_bank[bank], number).then_inc(aux_used, 1)
                                if number == 1:
                                    dve.wait_ge(aux_used, at + 1 + AUX)
                                    proj.stats(nc, link)
                            elif kind == "o":
                                if (s, step) == (3, 11):
                                    proj.normalise(nc, dve, link, i)
                                read_o(link, i, s - 1 if number == 1 else s, 0 if number == 0 else 1, at, bank)
                            else:
                                read_max(link, number, bank)
                                if number == MAXIMA - 1:
                                    split_max(link, at + 1 + AUX)

            with dve.Fori(0, ITERS - 1) as i:
                body(i, False)
            body(ITERS - 1, True)




class OutputGroup:

    G = 4
    LINKS = 2 + 5

    def __init__(self, nc, ctx, ar, prefix):
        G = self.G
        self.o_in = ar.take(2, G, P)
        self.sum_in = ar.take(G, DIM)
        self.oT = ar.take(G, KC, P)
        self.y = ar.take(G, DIM)
        self.wo = ar.take(KC, DIM)
        self.gamma = ar.take(DIM)
        self.beta = ar.take(DIM)
        self.bn = ar.take(G, 6)
        self.mv = ar.take(G, 2)
        self.var, self.guess, self.rstd, self.tmp = ar.take(G), ar.take(G), ar.take(G), ar.take(G)

        def sem(name):
            return ctx.enter_context(nc.semaphore(prefix + name))

        self.var_ready, self.guess_ready = sem("var_ready"), sem("guess_ready")
        self.normal_ready, self.pchain, self.y_ready = sem("normal_ready"), sem("group_pchain"), sem("y_ready")

    def load_consts(self, sp, w, done):
        sp.dma_start(self.wo, w["wo"]).then_inc(done, 16)
        sp.dma_start(self.gamma, w["gamma"].partition_broadcast(P)).then_inc(done, 16)
        sp.dma_start(self.beta, w["beta"].partition_broadcast(P)).then_inc(done, 16)

    def tokens(self, a, g):
        return a.rearrange("b (h t p) d -> (b h) p t d", p=P, t=self.G)[g]

    def load(self, sp, scratch, at, g, done):
        for half in range(2):
            src = scratch["o"].rearrange("(g a) t p d -> g a p t d", a=2)[at][half]
            sp.dma_start(self.o_in[:, half], src).then_inc(done, 16)
        sp.dma_start(self.sum_in, self.tokens(scratch["ffn"], g)).then_inc(done, 16)

    def store(self, sp, out, g, done):
        sp.dma_start(self.tokens(out, g), self.y).then_inc(done, 16)

    def turn(self, nc, bank, n, ident):
        for q in range(2):
            for kc in range(KC):
                at = (q * KC + kc) * P
                last = nc.tensor.transpose(bank[:, at:at + P], self.o_in[:, kc, 2 * n + q], ident)
        return last

    def project(self, nc, bank, n):
        for q in range(2):
            for kc in range(KC):
                last = nc.tensor.matmul(bank[:, q * DIM:(q + 1) * DIM], self.oT[:, 2 * n + q, kc], self.wo[:, kc],
                                        start=kc == 0, stop=kc == KC - 1)
        return last

    def read_turned(self, nc, bank, n):
        return nc.vector.tensor_copy(self.oT[:, 2 * n:2 * n + 2].rearrange("p a b c -> p (a b c)"), bank)

    def read_projected(self, nc, bank, n):
        return nc.vector.tensor_copy(self.y[:, 2 * n:2 * n + 2].rearrange("p a b -> p (a b)"), bank)

    def stats(self, nc, link):
        for q in range(self.G):
            ins = nc.vector.bn_stats(self.bn[:, q], self.y[:, q])
        link(ins)
        nc.vector.memset(self.tmp, 0.0)
        for q in range(self.G):
            ins = nc.vector.bn_aggr(self.mv[:, q], self.bn[:, q])
        link(ins)
        nc.vector.tensor_scalar(self.var, self.mv[:, :, 1], LN_EPS, None, ALU.add).then_inc(self.var_ready, 1)

    def normalise(self, nc, dve, link, n):
        dve.wait_ge(self.guess_ready, n + 1)
        rstd_newton(nc, link, self.rstd, self.var, self.guess, self.tmp)
        for q in range(self.G):
            ins = nc.vector.tensor_scalar(self.y[:, q], self.y[:, q], self.mv[:, q, 0:1], self.rstd[:, q:q + 1],
                                          ALU.subtract, ALU.mult)
        ins.then_inc(self.normal_ready, 1)

    def guess_std(self, nc):
        nc.scalar.activation(self.guess, self.var, ACT.Sqrt).then_inc(self.guess_ready, 1)

    def finish_pool(self, nc, pool, n):
        pool.wait_ge(self.normal_ready, n + 1)
        wide = [P, self.G, DIM]
        nc.gpsimd.tensor_tensor(self.y, self.y, self.gamma.unsqueeze(1).to_broadcast(wide), ALU.mult
                                ).then_inc(self.pchain, 1)
        pool.wait_ge(self.pchain, n * 2 + 1)
        nc.gpsimd.tensor_tensor(self.y, self.y, self.beta.unsqueeze(1).to_broadcast(wide), ALU.add
                                ).then_inc(self.pchain, 1)
        pool.wait_ge(self.pchain, n * 2 + 2)
        nc.gpsimd.tensor_tensor(self.y, self.y, self.sum_in, ALU.add).then_inc(self.y_ready, 1)




def last_groups_stage(nc, ctx, base, ps, w, scratch, out):
    ar = Arena(base)
    ident = ar.take(P)
    groups = [OutputGroup(nc, ctx, ar, f"o{h}_") for h in range(2)]

    def sem(name):
        return ctx.enter_context(nc.semaphore("o_" + name))

    ident_in, consts_in, stored, dchain = sem("ident_in"), sem("consts_in"), sem("stored"), sem("dchain")
    group_in = [sem(f"group{h}_in") for h in range(2)]
    turned, turned_read, projected, projected_read = (
        sem("turned"), sem("turned_read"), sem("projected"), sem("projected_read"))

    def bank(h, n):
        return ps[:, (4 * h + n) * CH:(4 * h + n + 1) * CH]

    with nc.Block() as block:

        @block.sync
        def _(sp):
            nc.sync.dma_start(ident, w["ident"]).then_inc(ident_in, 16)
            for h, g in enumerate(groups):
                g.load(nc.sync, scratch, 2 * BATCH + h, 2 * BATCH - 2 + h, group_in[h])
            for g in groups:
                g.load_consts(nc.sync, w, consts_in)
            for h, g in enumerate(groups):
                sp.wait_ge(g.y_ready, 1)
                g.store(nc.sync, out, 2 * BATCH - 2 + h, stored)
            sp.wait_ge(stored, 32)

        @block.tensor
        def _(pe):
            pe.wait_ge(ident_in, 16)
            for h, g in enumerate(groups):
                pe.wait_ge(group_in[h], 48)
                for n in range(2):
                    g.turn(nc, bank(h, n), n, ident).then_inc(turned, 1)
            pe.wait_ge(consts_in, 16 * 6)
            for h, g in enumerate(groups):
                for n in range(2):
                    pe.wait_ge(turned_read, 2 * h + n + 1)
                    g.project(nc, bank(h, 2 + n), n).then_inc(projected, 1)

        @block.scalar
        def _(act):
            for h, g in enumerate(groups):
                act.wait_ge(g.var_ready, 1)
                g.guess_std(nc)

        @block.gpsimd
        def _(pool):
            pool.wait_ge(consts_in, 16 * 6)
            for h, g in enumerate(groups):
                pool.wait_ge(group_in[h], 48)
                g.finish_pool(nc, pool, 0)

        @block.vector
        def _(dve):
            link = Chain(dve, dchain)
            for h, g in enumerate(groups):
                for n in range(2):
                    dve.wait_ge(turned, 2 * h + n + 1)
                    g.read_turned(nc, bank(h, n), n).then_inc(turned_read, 1)
            for h, g in enumerate(groups):
                for n in range(2):
                    dve.wait_ge(projected, 2 * h + n + 1)
                    g.read_projected(nc, bank(h, 2 + n), n).then_inc(projected_read, 1)
                dve.wait_ge(projected_read, 2 * h + 2)
                g.stats(nc, link)
            for g in groups:
                g.normalise(nc, dve, link, 0)




def leaf_path(leaf):
    cur, path = 0, []
    for depth in range(DEPTH - 1, -1, -1):
        side = leaf >> depth & 1
        path.append((cur, side))
        cur = 2 * cur + 1 + side
    return path


def tree_constants():
    count = np.zeros((P, P), np.float32)
    one = NFFF * NODES
    for f in range(NFFF):
        for leaf in range(LEAVES):
            for node, side in leaf_path(leaf):
                count[f * NODES + node, f * LEAVES + leaf] += -1.0 if side else 1.0
                if side:
                    count[one, f * LEAVES + leaf] += 1.0
    unit = np.repeat(count[:, :NFFF * LEAVES], LEAF_W, axis=1) * -BIG
    count[:, P // 2:] = count[:, :P // 2]
    return count, unit.reshape(P, NFFF, HT, P)


def build(nc, args):
    with ExitStack() as ctx:
        scratch = {
            "xnT": nc.dram_tensor("scratch_xnT", [BATCH, P, KC, SEQ], F32, kind="Internal").ap(),
            "ffn": nc.dram_tensor("scratch_ffn", [BATCH, SEQ, DIM], F32, kind="Internal").ap(),
            "split": nc.dram_tensor("scratch_split", [SETS // 2, 2, 3, P, SEQ], BF16, kind="Internal").ap(),
            "o": nc.dram_tensor("scratch_o", [4 * (BATCH + 1), TT // 2, P, P], F32, kind="Internal").ap(),
        }
        ps = ctx.enter_context(nc.psum_tensor("psum", [P, 8 * CH], F32))
        with ExitStack() as memory:
            ffn_stage(nc, memory, ps, args["x"], args, scratch)
        base = ctx.enter_context(nc.sbuf_tensor("arena", [P, ATTENTION_WORDS], F32))
        attention_stage(nc, ctx, base, ps, args, scratch, args["out"])
        last_groups_stage(nc, ctx, base, ps, args, scratch, args["out"])


def laid_out(inputs):
    bf16 = mybir.dt.np(BF16)
    a = {k: np.asarray(v) for k, v in inputs.items()}
    att = {k[len("L0_attn_"):]: v for k, v in a.items() if k.startswith("L0_attn_")}
    ffn = [{k[len("L0_ffn_q_"):]: v for k, v in a.items() if k.startswith(f"L0_ffn_{f}_")} for f in "qkv"]

    def chunks(m):
        return m.reshape(-1, P, m.shape[1]).transpose(1, 0, 2)

    wq, wk, wv = (chunks(att[k]) for k in ("Wq", "Wk", "Wv"))
    count, unit = tree_constants()
    b2 = np.zeros((P, NFFF, DIM), np.float32)
    for f in range(NFFF):
        for half in range(2):
            at = half * P // 2 + f * LEAVES
            b2[at:at + LEAVES, f] = ffn[f]["b2"]
    pick = np.zeros((3 * PARTS, PARTS, SEQ), np.float32)
    for j in range(PARTS):
        pick[3 * j:3 * j + 3, j] = 1.0
    return {
        "x": att["x"],
        "wqk": np.stack([np.stack([wq[:, :, t * P:(t + 1) * P], wk[:, :, t * P:(t + 1) * P]], 2) for t in range(4)]),
        "wv": np.stack([wv[:, :, t * 64:(t + 1) * 64] for t in range(4)]),
        "wo": chunks(att["Wo"]),
        "lq1": att["lambda_q1"], "lk1": att["lambda_k1"], "lq2": att["lambda_q2"], "lk2": att["lambda_k2"],
        "gamma": att["gamma"], "beta": att["beta"],
        "nodeT": chunks(np.concatenate([p["node_w"].T for p in ffn], 1)),
        "nodeb": np.concatenate([p["node_b"] for p in ffn])[:, None],
        "w1": np.stack([chunks(p["w1"].transpose(1, 0, 2).reshape(DIM, HID)) for p in ffn]),
        "w2": np.stack([chunks(p["w2"].reshape(HID, DIM)) for p in ffn]),
        "b1": np.concatenate([p["b1"].reshape(HT, P).T for p in ffn], 1),
        "b2": b2,
        "off_leaf": unit.astype(bf16),
        "off_count": count.astype(bf16),
        "pick": pick.astype(bf16),
        "ident": np.eye(P, dtype=np.float32),
        "identb": np.eye(P, dtype=np.float32).astype(bf16),
    }


def kernel(**inputs):
    import concourse.bacc as _bacc
    from concourse.bass_utils import run_bass_kernel_spmd as _run

    nc = _bacc.Bacc("TRN2", target_bir_lowering=False, num_devices=1)
    arrays, args = {}, {}
    for name, value in laid_out(inputs).items():
        value = np.ascontiguousarray(value)
        arrays[f"in_{name}"] = value
        args[name] = nc.dram_tensor(f"in_{name}", value.shape, mybir.dt.from_np(value.dtype),
                                    kind="ExternalInput").ap()
    args["out"] = nc.dram_tensor("out_0", (BATCH, SEQ, DIM), F32, kind="ExternalOutput").ap()
    build(nc, args)
    r = _run(nc, [arrays], core_ids=[0])
    return r.results[0]["out_0"]
```
